# Optimizing a Trainium2 kernel written in Bass

```python
import numpy as np
import jax
import jax.numpy as jnp

def _softmax(x, axis=-1):
    return jax.nn.softmax(x, axis=axis)

def _gelu(x):
    return jax.nn.gelu(x, approximate=True)

def _silu(x):
    return jax.nn.silu(x)

def _sigmoid(x):
    return jax.nn.sigmoid(x)

def _layernorm(x, axis=-1, eps=1e-05):
    m = jnp.mean(x, axis=axis, keepdims=True)
    v = jnp.var(x, axis=axis, keepdims=True)
    return (x - m) / jnp.sqrt(v + eps)

def _scatter_add(tgt, idx, src, axis=0):
    return tgt.at[idx].add(src)

def _segment_sum(src, seg, n):
    return jax.ops.segment_sum(src, seg, n)
kernel_name = 'mk_gnn_resnorm_d2_gnn_r8_671440'

def setup_inputs(seed: int=0):
    np.random.seed(seed)
    _w = jnp.asarray

    def _rec_inputs():
        import jax
        import jax.numpy as jnp
        _gk = jax.random.key(seed)
        x = -0.0006008 + 1.001 * jax.random.normal(jax.random.fold_in(_gk, 1), (6250, 256), jnp.float32)
        _s = jax.random.randint(jax.random.fold_in(_gk, 2), (100000,), 0, 6250, jnp.int32)
        _d = jax.random.randint(jax.random.fold_in(_gk, 3), (100000,), 0, 6250, jnp.int32)
        _loop = jnp.arange(6250, dtype=jnp.int32)
        src = jnp.concatenate([_s, _d, _loop])
        dst = jnp.concatenate([_d, _s, _loop])
        _o = jnp.argsort(dst, stable=True)
        src = src[_o]
        dst = dst[_o]
        edge_attr_64 = -9.77346e-05 + 0.999888 * jax.random.normal(jax.random.fold_in(_gk, 12), (206250, 64), jnp.float32)
        edge_type_16 = jax.random.randint(jax.random.fold_in(_gk, 13), (206250,), 0, 16, jnp.int32)
        return (x, src, dst, edge_attr_64, edge_type_16)
    x, src, dst, edge_attr_64, edge_type_16 = _rec_inputs()

    def _L0_gnn_setup():
        import jax, jax.numpy as jnp
        import numpy as np
        from jax.ops import segment_sum
        N_NODES = 1250
        N_EDGES = 20000
        IN_FEAT = 256
        OUT_FEAT = 256
        NUM_RELS = 16

        def _inv_degree(idx, n):
            deg = segment_sum(jnp.ones(idx.shape[0], dtype=jnp.float32), idx, num_segments=n)
            return jnp.where(deg > 0, 1.0 / deg, 0.0)

        def _typed_pass(feat, W, bias, src_idx, dst_idx, etypes, norm_per_edge, n):
            proj = jnp.einsum('ni,rio->rno', feat, W)
            m = proj[etypes, src_idx] + bias
            m = m * norm_per_edge[:, None]
            return segment_sum(m, dst_idx, num_segments=n)
        key = jax.random.key(seed)
        ks = jax.random.split(key, 8)
        feat = jax.random.normal(ks[0], (N_NODES, IN_FEAT), dtype=jnp.float32)
        Wf = jax.random.normal(ks[1], (NUM_RELS, IN_FEAT, OUT_FEAT), dtype=jnp.float32)
        Wb = jax.random.normal(ks[2], (NUM_RELS, IN_FEAT, OUT_FEAT), dtype=jnp.float32)
        loop_weight = jax.random.normal(ks[3], (IN_FEAT, OUT_FEAT), dtype=jnp.float32)
        forward_bias = jnp.zeros((OUT_FEAT,), dtype=jnp.float32)
        backward_bias = jnp.zeros((OUT_FEAT,), dtype=jnp.float32)
        self_bias = jnp.zeros((OUT_FEAT,), dtype=jnp.float32)
        src = jax.random.randint(ks[4], (N_EDGES,), 0, N_NODES, dtype=jnp.int32)
        dst = jax.random.randint(ks[5], (N_EDGES,), 0, N_NODES, dtype=jnp.int32)
        etypes = jax.random.randint(ks[6], (N_EDGES,), 0, NUM_RELS, dtype=jnp.int32)
        return {'feat': feat, 'Wf': Wf, 'Wb': Wb, 'loop_weight': loop_weight, 'forward_bias': forward_bias, 'backward_bias': backward_bias, 'self_bias': self_bias, 'src': src, 'dst': dst, 'etypes': etypes, 'use_dis_weight': 0, 'drop_out': 0}
    _L0_gnn_all = _L0_gnn_setup()
    _L0_gnn_in = {k: v for k, v in _L0_gnn_all.items() if k in ('Wf', 'Wb', 'loop_weight', 'forward_bias', 'backward_bias', 'self_bias')}
    del _L0_gnn_all

    def _L1_gnn_setup():
        import jax, jax.numpy as jnp
        import numpy as np
        ALPHA = 0.2
        key = jax.random.key(seed)
        ks = jax.random.split(key, 6)
        N, E, F_IN, F_OUT, E_DIM = (6250, 100000, 256, 256, 64)
        h = jax.random.normal(ks[0], (N, F_IN), dtype=jnp.float32)
        e_feat = jax.random.normal(ks[1], (E, E_DIM), dtype=jnp.float32)
        W = jax.random.normal(ks[2], (F_OUT, F_IN), dtype=jnp.float32) * (1.0 / np.sqrt(F_IN))
        A = jax.random.normal(ks[3], (1, 2 * F_OUT + E_DIM), dtype=jnp.float32) * 0.05
        src = jax.random.randint(ks[4], (E,), 0, N, dtype=jnp.int32)
        dst = jax.random.randint(ks[5], (E,), 0, N, dtype=jnp.int32)
        return {'h': h, 'e_feat': e_feat, 'W': W, 'A': A, 'src': src, 'dst': dst}
    _L1_gnn_all = _L1_gnn_setup()
    _L1_gnn_in = {k: v for k, v in _L1_gnn_all.items() if k in ('W', 'A')}
    del _L1_gnn_all
    return {'x': x, 'src': src, 'dst': dst, 'edge_attr_64': edge_attr_64, 'edge_type_16': edge_type_16, 'L0_gnn_Wf': _L0_gnn_in['Wf'], 'L0_gnn_Wb': _L0_gnn_in['Wb'], 'L0_gnn_loop_weight': _L0_gnn_in['loop_weight'], 'L0_gnn_forward_bias': _L0_gnn_in['forward_bias'], 'L0_gnn_backward_bias': _L0_gnn_in['backward_bias'], 'L0_gnn_self_bias': _L0_gnn_in['self_bias'], 'L1_gnn_W': _L1_gnn_in['W'], 'L1_gnn_A': _L1_gnn_in['A']}

def reference(x, src, dst, edge_attr_64, edge_type_16, L0_gnn_Wf, L0_gnn_Wb, L0_gnn_loop_weight, L0_gnn_forward_bias, L0_gnn_backward_bias, L0_gnn_self_bias, L1_gnn_W, L1_gnn_A):
    import jax
    import jax.numpy as jnp

    def _L0_gnn_ref(feat, Wf, Wb, loop_weight, forward_bias, backward_bias, self_bias, src, dst, etypes, use_dis_weight, drop_out):
        import jax, jax.numpy as jnp
        import numpy as np
        from jax.ops import segment_sum
        N_NODES = 1250
        N_EDGES = 20000
        IN_FEAT = 256
        OUT_FEAT = 256
        NUM_RELS = 16

        def _inv_degree(idx, n):
            deg = segment_sum(jnp.ones(idx.shape[0], dtype=jnp.float32), idx, num_segments=n)
            return jnp.where(deg > 0, 1.0 / deg, 0.0)

        def _typed_pass(feat, W, bias, src_idx, dst_idx, etypes, norm_per_edge, n):
            proj = jnp.einsum('ni,rio->rno', feat, W)
            m = proj[etypes, src_idx] + bias
            m = m * norm_per_edge[:, None]
            return segment_sum(m, dst_idx, num_segments=n)
        n = feat.shape[0]
        norm_f = _inv_degree(dst, n)[dst]
        m_forward = _typed_pass(feat, Wf, forward_bias, src, dst, etypes, norm_f, n)
        norm_b = _inv_degree(src, n)[src]
        m_backward = _typed_pass(feat, Wb, backward_bias, dst, src, etypes, norm_b, n)
        s = feat @ loop_weight
        s = s + s + self_bias
        return s + m_forward + m_backward

    def _L1_gnn_ref(h, e_feat, W, A, src, dst):
        import jax, jax.numpy as jnp
        import numpy as np
        ALPHA = 0.2
        N = h.shape[0]
        F_OUT = W.shape[0]
        z = h @ W.T
        z_src = z[src]
        z_dst = z[dst]
        a_src, a_dst, a_e = (A[0, :F_OUT], A[0, F_OUT:2 * F_OUT], A[0, 2 * F_OUT:])
        logits = z_src @ a_src + z_dst @ a_dst + e_feat @ a_e
        e = jax.nn.leaky_relu(logits, ALPHA)
        m = jax.ops.segment_max(e, dst, num_segments=N)
        ex = jnp.exp(e - m[dst])
        denom = jax.ops.segment_sum(ex, dst, num_segments=N)
        alpha = ex / denom[dst]
        h_out = jax.ops.segment_sum(alpha[:, None] * z_src, dst, num_segments=N)
        return h_out
    x = _layernorm(x + _L0_gnn_ref(x, L0_gnn_Wf, L0_gnn_Wb, L0_gnn_loop_weight, L0_gnn_forward_bias, L0_gnn_backward_bias, L0_gnn_self_bias, src, dst, edge_type_16, 0, 0), axis=-1)
    x = _layernorm(x + _L1_gnn_ref(x, edge_attr_64, L1_gnn_W, L1_gnn_A, src, dst), axis=-1)
    return x

_drawn_inputs = setup_inputs


def setup_inputs(seed=0):
    import zlib

    import numpy as np

    out = dict(_drawn_inputs(seed))
    spreads = {'L0_gnn_forward_bias': (0.0, 0.8),
     'L0_gnn_backward_bias': (0.0, 0.8),
     'L0_gnn_self_bias': (0.0, 0.8)}
    factors = {}
    for name, (base, spread) in spreads.items():
        noise = np.random.default_rng([zlib.crc32(name.encode()), seed]).standard_normal(out[name].shape)
        drawn = base * np.exp(spread * noise) if base else spread * noise
        out[name] = jnp.asarray(drawn.astype(out[name].dtype))
    for name, factor in factors.items():
        out[name] = (out[name] * factor).astype(out[name].dtype)
    return out
```

```python
from contextlib import ExitStack

import concourse.bass as bass
from concourse import mybir

P = 128
F32 = mybir.dt.float32
I32 = mybir.dt.int32
U32 = mybir.dt.uint32
U16 = mybir.dt.uint16
ALU = mybir.AluOpType
ACT = mybir.ActivationFunctionType
AX = mybir.AxisListType

EDGE_ROWS = 125
HALF = 15
RING = 16
GROUP = 4
BANKS = 4
ROW = 260
COUNT = 256
DENOM = 257
NEG_MAX = 258
S_DST = 259
EPS = 1e-5
ALPHA = 0.2
FAR = 1e30
FLOOR = 1e28


class Tally:

    def __init__(self, sem):
        self.sem, self.n = sem, 0

    def up(self, instruction):
        instruction.then_inc(self.sem, 1)
        self.n += 1


def gnn(nc, x_pad, xT_pad, src, dst, edge_attr, edge_type, Wf, Wb, loop_weight, forward_bias,
        backward_bias, self_bias, W1, W1T, A1, out):
    NPAD, D = x_pad.shape
    E, ED = edge_attr.shape
    R = Wf.shape[0]
    KC = D // P
    NT = NPAD // P
    EC = E // EDGE_ROWS
    assert EC * EDGE_ROWS == E and EC % (2 * HALF) == 0 and D == 2 * P and R * D % 1024 == 0
    EDGE_TILES = (E + NT * (P - 1)) // P
    TC = -(-EDGE_TILES // P)
    T = TC * P
    SCATTER_STEPS = EC // (2 * HALF)
    EDGE_STEPS = max(2, SCATTER_STEPS // 5)
    CHUNK = EC // (2 * EDGE_STEPS)
    PAIRS = (NT - 1) // 2
    assert CHUNK * 2 * EDGE_STEPS == EC and PAIRS > 1
    HALF_W = R * D // 2
    BLOCKS = HALF_W // 512

    table_f = nc.dram_tensor("table_f", (NPAD, R * D), F32)
    table_b = nc.dram_tensor("table_b", (NPAD, R * D), F32)
    z_table = nc.dram_tensor("z_table", (NPAD, DENOM + 1), F32)
    slots_b = nc.dram_tensor("slots_b", (P * T, 2), F32)
    slots_f = nc.dram_tensor("slots_f", (P * T, 4), F32)
    owner_b = nc.dram_tensor("owner_b", (T,), I32)
    owner_f = nc.dram_tensor("owner_f", (T,), I32)

    with ExitStack() as whole:
        def sem(name):
            return whole.enter_context(nc.semaphore(name))

        def sb(name, shape, dt=F32, scope=whole):
            return scope.enter_context(nc.sbuf_tensor(name, shape, dt))

        def psum(name, shape, scope):
            return scope.enter_context(nc.psum_tensor(name, shape, F32))

        iota = sb("iota", [P, P])
        iota_i = sb("iota_i", [P, P], I32)
        row_i = sb("row_i", [P, 1], I32)
        row_f = sb("row_f", [P, 1])
        ident = sb("ident", [P, P])

        with ExitStack() as one:
            def s1(name, shape, dt=F32):
                return sb(name, shape, dt, one)

            src_i = s1("src_i", [EDGE_ROWS, EC], I32)
            dst_i = s1("dst_i", [EDGE_ROWS, EC], I32)
            type_i = s1("type_i", [EDGE_ROWS, EC], I32)
            feat = s1("feat", [EDGE_ROWS, 2, CHUNK, ED])
            a_edge = s1("a_edge", [EDGE_ROWS, ED])
            work_i = s1("work_i", [EDGE_ROWS, EC], I32)
            bucket = s1("bucket", [EDGE_ROWS, EC])
            inside = s1("inside", [EDGE_ROWS, EC], U16)
            ranks = s1("ranks", [EDGE_ROWS, EC])
            place = s1("place", [EDGE_ROWS, EC])
            nil = s1("nil", [EDGE_ROWS, EC])
            addr = [s1("addr_b", [EDGE_ROWS, EC], U32), s1("addr_f", [EDGE_ROWS, EC], U32)]
            recs = [s1("recs_b", [EDGE_ROWS, EC, 2]), s1("recs_f", [EDGE_ROWS, EC, 4])]
            below = s1("below", [EDGE_ROWS, P])
            ones = s1("ones", [EDGE_ROWS, P])
            tile_i = s1("tile_i", [P, TC], I32)
            tile_f = s1("tile_f", [P, TC])
            count = s1("count", [EDGE_ROWS, NT])
            tiles_i = s1("tiles_i", [P, NT], I32)
            tiles = s1("tiles", [P, NT])
            tend = s1("tend", [P, NT])
            base = s1("base", [P, NT])
            past = s1("past", [P, TC, NT])
            owner = s1("owner", [P, TC])
            owner_i = [s1("owner_ib", [P, TC], I32), s1("owner_if", [P, TC], I32)]
            blank_b = s1("blank_b", [P, TC, 2])
            blank_f = s1("blank_f", [P, TC, 4])
            w_rel = s1("w_rel", [P, KC, R, D])
            xT = s1("xT", [P, 2, KC, P])
            proj = s1("proj", [P, 2, HALF_W])
            stage_rec = [s1("stage_recb", [EDGE_ROWS, 2, HALF, 2]), s1("stage_recf", [EDGE_ROWS, 2, HALF, 4])]
            stage_addr = s1("stage_addr", [EDGE_ROWS, 2, HALF], U32)
            ps_proj = psum("ps_proj", [P, BANKS, 512], one)
            ps_count = psum("ps_count", [P, 512], one)[:, 0:4 * NT].rearrange("p (w k t) -> p w k t", w=2, k=2)

            keys_landed = sem("keys_landed")
            type_landed = sem("type_landed")
            a_edge_landed = sem("a_edge_landed")
            feat_landed = [sem("feat_landed0"), sem("feat_landed1")]
            feat_used = sem("feat_used")
            iotas = sem("iotas")
            blanks = sem("blanks")
            blank_stored = sem("blank_stored")
            vdone = sem("vdone")
            counted = [sem("counted_b"), sem("counted_f")]
            count_summed = [sem("count_summed_b"), sem("count_summed_f")]
            owner_made = sem("owner_made")
            owner_stored = sem("owner_stored")
            placed = [sem("placed_b"), sem("placed_f")]
            features_dotted = sem("features_dotted")
            staged = [sem("scatter_staged0"), sem("scatter_staged1")]
            scattered = [sem("scattered0"), sem("scattered1")]
            w_landed = sem("w_landed")
            xT_landed = [sem("xT_landed0"), sem("xT_landed1")]
            proj_summed = sem("proj_summed")
            proj_copied = sem("proj_copied")
            proj_stored = [sem("proj_stored0"), sem("proj_stored1")]

            block = one.enter_context(nc.Block())

            @block.sync
            def _(sp):
                sp.dma_start(src_i[:, :], src.rearrange("(p c) -> p c", c=EC)).then_inc(keys_landed, 16)
                sp.dma_start(dst_i[:, :], dst.rearrange("(p c) -> p c", c=EC)).then_inc(keys_landed, 16)
                sp.dma_start(type_i[:, :], edge_type.rearrange("(p c) -> p c", c=EC)).then_inc(type_landed, 16)
                sp.dma_start(a_edge[:, :], A1[:, 2 * D:].to_broadcast([EDGE_ROWS, ED])).then_inc(a_edge_landed, 16)
                sp.wait_ge(blanks, 4)
                blank_rows_b = slots_b.ap().rearrange("(p t) w -> p t w", t=T)
                blank_rows_f = slots_f.ap().rearrange("(p t) w -> p t w", t=T)
                for c in range(T // TC):
                    here = slice(c * TC, (c + 1) * TC)
                    sp.dma_start(blank_rows_b[:, here, :], blank_b[:, :, :]).then_inc(blank_stored, 16)
                    sp.dma_start(blank_rows_f[:, here, :], blank_f[:, :, :]).then_inc(blank_stored, 16)

                feat_rows = edge_attr.rearrange("(p c) f -> p c f", c=EC)

                def load_features(step, half):
                    sp.dma_start(feat[:, half, :, :], feat_rows[:, bass.ds(step * 2 * CHUNK + half * CHUNK, CHUNK), :])\
                        .then_inc(feat_landed[half], 16)

                def stage(way, step, half):
                    c0 = step * 2 * HALF + half * HALF
                    sp.dma_start(stage_rec[way][:, half, :, :], recs[way][:, bass.ds(c0, HALF), :]).then_inc(staged[half], 16)
                    sp.dma_start(stage_addr[:, half, :], addr[way][:, bass.ds(c0, HALF)]).then_inc(staged[half], 16)

                load_features(0, 0)
                load_features(0, 1)
                sp.wait_ge(placed[0], 1)
                stage(0, 0, 0)
                stage(0, 0, 1)
                with sp.Fori(1, EDGE_STEPS) as step:
                    for half in range(2):
                        sp.wait_ge(scattered[half], step * 16 * HALF)
                        stage(0, step, half)
                    for half in range(2):
                        sp.wait_ge(feat_used, step * 2 + (half - 1))
                        load_features(step, half)
                with sp.Fori(EDGE_STEPS, SCATTER_STEPS) as step:
                    for half in range(2):
                        sp.wait_ge(scattered[half], step * 16 * HALF)
                        stage(0, step, half)
                sp.wait_ge(placed[1], 1)
                sp.wait_ge(features_dotted, 1)
                with sp.Fori(0, SCATTER_STEPS) as step:
                    for half in range(2):
                        sp.wait_ge(scattered[half], (step + SCATTER_STEPS) * 16 * HALF)
                        stage(1, step, half)
                sp.wait_ge(owner_stored, 32)

            @block.gpsimd
            def _(pool):
                pool.iota(iota_i[:, :], pattern=[[1, P]], base=0, channel_multiplier=0).then_inc(iotas, 1)
                pool.iota(row_i[:, :], pattern=[[0, 1]], base=0, channel_multiplier=1).then_inc(iotas, 1)
                pool.iota(tile_i[:, :], pattern=[[1, TC]], base=0, channel_multiplier=TC).then_inc(iotas, 1)
                pool.memset(blank_b[:, :, 0], 0.0).then_inc(blanks, 1)
                pool.memset(blank_b[:, :, 1], -1.0).then_inc(blanks, 1)
                pool.memset(blank_f[:, :, 0:4], 0.0).then_inc(blanks, 1)
                pool.wait_ge(blanks, 3)
                pool.memset(blank_f[:, :, 1], -1.0).then_inc(blanks, 1)
                pool.wait_ge(blank_stored, 32 * (T // TC))
                for way, slots in ((0, slots_b), (1, slots_f)):
                    def scatter(half):
                        for c in range(HALF):
                            pool.indirect_dma_start(
                                slots.ap(), bass.IndirectOffsetOnAxis(ap=stage_addr[:, half, c:c + 1], axis=0),
                                stage_rec[way][:, half, c, :], None).then_inc(scattered[half], 16)

                    with pool.Fori(0, SCATTER_STEPS) as step:
                        for half in range(2):
                            pool.wait_ge(staged[half], step * 32 + (way * SCATTER_STEPS + 1) * 32)
                            pool.nop(nofuse=True)
                            scatter(half)
                for half in range(2):
                    pool.wait_ge(scattered[half], 2 * SCATTER_STEPS * HALF * 16)

            @block.vector
            def _(dve):
                v = Tally(vdone)
                dve.wait_ge(iotas, 3)
                v.up(dve.tensor_copy(iota[:, :], iota_i[:, :]))
                v.up(dve.tensor_copy(row_f[:, :], row_i[:, :]))
                v.up(dve.tensor_copy(tile_f[:, :], tile_i[:, :]))
                v.up(dve.memset(ones[:, :], 1.0))
                v.up(dve.memset(nil[:, :], 0.0))
                dve.wait_ge(vdone, v.n)
                v.up(dve.tensor_scalar(ident[:, :], iota[:, :], row_f[:, 0:1], None, ALU.is_equal))
                v.up(dve.tensor_scalar(below[:, :], iota[0:EDGE_ROWS, :], row_f[0:EDGE_ROWS, 0:1], None, ALU.is_gt))
                dve.wait_ge(keys_landed, 32)
                for way, key, other in ((0, src_i, dst_i), (1, dst_i, src_i)):
                    dve.wait_ge(vdone, v.n)
                    v.up(dve.tensor_scalar(work_i[:, :], key[:, :], 7, None, ALU.logical_shift_right))
                    dve.wait_ge(vdone, v.n)
                    v.up(dve.tensor_copy(bucket[:, :], work_i[:, :]))
                    dve.wait_ge(vdone, v.n)
                    v.up(dve.tensor_scalar(work_i[:, :], key[:, :], P - 1, None, ALU.bitwise_and))
                    dve.wait_ge(vdone, v.n)
                    v.up(dve.tensor_copy(recs[way][:, :, 1], work_i[:, :]))
                    n = v.n
                    with dve.Fori(0, NT) as b:
                        dve.wait_ge(vdone, b + n)
                        dve.tensor_scalar(inside[:, :], bucket[:, :], iota[0:EDGE_ROWS, bass.ds(b, 1)], None,
                                          ALU.is_equal, ALU.add, accum_out=count[:, bass.ds(b, 1)]).then_inc(vdone, 1)
                    v.n += NT
                    dve.wait_ge(vdone, v.n)
                    dve.sem_inc(counted[way], 1)
                    dve.wait_ge(count_summed[way], 1)
                    v.up(dve.tensor_scalar(tiles[:, :], ps_count[:, way, 0, :], float(P - 1), None, ALU.add))
                    dve.wait_ge(vdone, v.n)
                    v.up(dve.tensor_copy(tiles_i[:, :], tiles[:, :]))
                    dve.wait_ge(vdone, v.n)
                    v.up(dve.tensor_scalar(tiles_i[:, :], tiles_i[:, :], 7, None, ALU.logical_shift_right))
                    dve.wait_ge(vdone, v.n)
                    v.up(dve.tensor_copy(tiles[:, :], tiles_i[:, :]))
                    dve.wait_ge(vdone, v.n)
                    v.up(dve.memset(base[:, :], 0.0))
                    v.up(dve.memset(place[:, :], 1.0))
                    dve.wait_ge(vdone, v.n)
                    v.up(dve.tensor_tensor_scan(tend[:, :], tiles[:, :], base[:, :], 0.0, ALU.add, ALU.add))
                    dve.wait_ge(vdone, v.n)
                    v.up(dve.tensor_sub(base[:, :], tend[:, :], tiles[:, :]))
                    dve.wait_ge(vdone, v.n)
                    v.up(dve.scalar_tensor_tensor(base[:, :], base[:, :], float(P), ps_count[:, way, 1, :], ALU.mult, ALU.add))
                    n = v.n
                    with dve.Fori(0, NT) as b:
                        dve.wait_ge(vdone, b * 3 + n)
                        dve.tensor_scalar(inside[:, :], bucket[:, :], iota[0:EDGE_ROWS, bass.ds(b, 1)], None,
                                          ALU.is_equal).then_inc(vdone, 1)
                        dve.wait_ge(vdone, b * 3 + (n + 1))
                        dve.tensor_tensor_scan(ranks[:, :], inside[:, :], nil[:, :], base[0:EDGE_ROWS, bass.ds(b, 1)],
                                               ALU.add, ALU.add).then_inc(vdone, 1)
                        dve.wait_ge(vdone, b * 3 + (n + 2))
                        dve.nop(nofuse=True)
                        dve.copy_predicated(place[:, :], inside[:, :], ranks[:, :]).then_inc(vdone, 1)
                    v.n += 3 * NT
                    dve.wait_ge(vdone, v.n)
                    v.up(dve.tensor_scalar(work_i[:, :], place[:, :], -1.0, None, ALU.add))
                    dve.wait_ge(vdone, v.n)
                    v.up(dve.tensor_scalar(ranks[:, :].bitcast(I32), work_i[:, :], P - 1, None, ALU.bitwise_and))
                    v.up(dve.tensor_scalar(place[:, :].bitcast(I32), work_i[:, :], 7, None, ALU.logical_shift_right))
                    dve.wait_ge(vdone, v.n)
                    v.up(dve.scalar_tensor_tensor(addr[way][:, :], ranks[:, :].bitcast(I32), float(T), place[:, :].bitcast(I32),
                                                  ALU.mult, ALU.add))
                    if way == 0:
                        dve.wait_ge(type_landed, 16)
                    v.up(dve.scalar_tensor_tensor(recs[way][:, :, 0], other[:, :], float(R), type_i[:, :], ALU.mult, ALU.add))
                    if way == 1:
                        v.up(dve.tensor_copy(recs[way][:, :, 2], other[:, :]))
                    dve.wait_ge(vdone, v.n)
                    dve.sem_inc(placed[way], 1)
                    v.up(dve.tensor_tensor(past[:, :, :], tile_f[:, :].unsqueeze(2).to_broadcast([P, TC, NT]),
                                           tend[:, :].unsqueeze(1).to_broadcast([P, TC, NT]), ALU.is_ge))
                    dve.wait_ge(vdone, v.n)
                    v.up(dve.tensor_reduce(owner[:, :], past[:, :, :], AX.X, ALU.add))
                    dve.wait_ge(vdone, v.n)
                    v.up(dve.tensor_scalar(owner_i[way][:, :], owner[:, :], float(NT - 1), float(ROW), ALU.min, ALU.mult))
                    dve.wait_ge(vdone, v.n)
                    dve.sem_inc(owner_made, 1)
                    if way == 0:
                        dve.wait_ge(a_edge_landed, 16)

                        n = v.n
                        with dve.Fori(0, EDGE_STEPS) as step:
                            for half in range(2):
                                dve.wait_ge(feat_landed[half], step * 16 + 16)
                                dve.tensor_tensor(feat[:, half, :, :], feat[:, half, :, :],
                                                  a_edge[:, :].unsqueeze(1).to_broadcast([EDGE_ROWS, CHUNK, ED]),
                                                  ALU.mult).then_inc(vdone, 1)
                                dve.wait_ge(vdone, step * 2 + (n + half + 1))
                                dve.tensor_reduce(recs[1][:, bass.ds(step * 2 * CHUNK + half * CHUNK, CHUNK), 3],
                                                  feat[:, half, :, :], AX.X, ALU.add).then_inc(feat_used, 1)
                        v.n += 2 * EDGE_STEPS
                        dve.wait_ge(feat_used, 2 * EDGE_STEPS)
                        dve.sem_inc(features_dotted, 1)

            @block.tensor
            def _(pe):
                def sum_counts(way):
                    pe.wait_ge(counted[way], 1)
                    nc.tensor.matmul(ps_count[:, way, 0, :], ones[:, :], count[:, :], start=True, stop=True)
                    nc.tensor.matmul(ps_count[:, way, 1, :], below[:, :], count[:, :], start=True, stop=True)\
                        .then_inc(count_summed[way], 1)

                def project(way, pair, buf):
                    t = pair * 2 + (way * NT + buf)
                    seen = (NT + 1 - buf) // 2 * way + 1
                    pe.wait_ge(xT_landed[buf], pair * 16 + seen * 16)
                    for g in range(2 * BLOCKS):
                        pe.wait_ge(proj_copied, t * (2 * BLOCKS) + (g + 1))
                        for k in range(KC):
                            r0 = g * 512 // D
                            last = nc.tensor.matmul(ps_proj[:, g % BANKS, :], xT[:, buf, k, :],
                                                    w_rel[:, k, r0:r0 + 512 // D, :], start=(k == 0), stop=(k == KC - 1))
                        last.then_inc(proj_summed, 1)

                for way in range(2):
                    sum_counts(way)
                    pe.wait_ge(w_landed, 16 * KC * (way + 1))
                    with pe.Fori(0, PAIRS) as pair:
                        project(way, pair, 0)
                        project(way, pair, 1)
                    for t in range(2 * PAIRS, NT):
                        project(way, t // 2, t % 2)

            @block.scalar
            def _(act):
                act.sem_inc(proj_copied, BANKS)
                for way, w, table in ((0, Wb, table_b), (1, Wf, table_f)):
                    if way:
                        act.wait_ge(proj_summed, NT * 2 * BLOCKS)
                    for k in range(KC):
                        act.dma_start(w_rel[:, k, :, :], w[:, k * P:(k + 1) * P, :].rearrange("r i o -> i r o"))\
                            .then_inc(w_landed, 16)

                    def load_x(pair, buf):
                        act.dma_start(xT[:, buf, :, :], xT_pad[:, bass.ds(pair * 2 * P + buf * P, P)].rearrange("(k p) n -> p k n", p=P))\
                            .then_inc(xT_landed[buf], 16)

                    def tile(pair, buf, first, last):
                        t = pair * 2 + (way * NT + buf)
                        if not last:
                            load_x(pair + buf, 1 - buf)
                        for half in range(2):
                            if not first:
                                act.wait_ge(proj_stored[half], t * 16)
                            for g in range(half * BLOCKS, (half + 1) * BLOCKS):
                                act.wait_ge(proj_summed, t * (2 * BLOCKS) + (g + 1))
                                act.activation(proj[:, half, (g % BLOCKS) * 512:(g % BLOCKS + 1) * 512],
                                               ps_proj[:, g % BANKS, :], ACT.Copy).then_inc(proj_copied, 1)
                            act.wait_ge(proj_copied, t * (2 * BLOCKS) + ((half + 1) * BLOCKS + BANKS))
                            act.dma_start(table.ap()[bass.ds(pair * 2 * P + buf * P, P), half * HALF_W:(half + 1) * HALF_W],
                                          proj[:, half, :]).then_inc(proj_stored[half], 16)

                    load_x(0, 0)
                    tile(0, 0, way == 0, False)
                    tile(0, 1, False, False)
                    with act.Fori(1, PAIRS) as pair:
                        tile(pair, 0, False, False)
                        tile(pair, 1, False, False)
                    for t in range(2 * PAIRS, NT):
                        tile(t // 2, t % 2, False, t == NT - 1)
                for half in range(2):
                    act.wait_ge(proj_stored[half], 2 * NT * 16)
                act.wait_ge(owner_made, 2)
                act.dma_start(owner_b.ap().rearrange("(p c) -> p c", c=TC), owner_i[0][:, :]).then_inc(owner_stored, 16)
                act.dma_start(owner_f.ap().rearrange("(p c) -> p c", c=TC), owner_i[1][:, :]).then_inc(owner_stored, 16)


        slots_sb_b = sb("slots_sb_b", [P, T, 2])
        slots_sb_f = sb("slots_sb_f", [P, T, 4])
        owner_sb = [sb("owner_sb_b", [1, T], I32), sb("owner_sb_f", [1, T], I32)]
        acc_b = sb("acc_b", [P, NT * ROW])
        acc_f = sb("acc_f", [P, NT * ROW])
        rows_b = acc_b[:, :].rearrange("p (t w) -> p t w", w=ROW)
        rows_f = acc_f[:, :].rearrange("p (t w) -> p t w", w=ROW)

        with ExitStack() as two:
            gathered = sb("gathered", [P, RING, ROW], scope=two)
            index = sb("index", [P, RING], U32, two)
            local = sb("local", [P, RING], scope=two)
            dot_e = sb("dot_e", [P, RING], scope=two)
            slots_landed = sem("slots_landed")

            def add_messages(way, slots_sb, table, acc):
                with ExitStack() as scope:
                    name = "fb"[1 - way]
                    match = sb("match" + name, [P, RING, P], scope=scope)
                    ps_sum = psum("ps_sum" + name, [P, BANKS, 512], scope)
                    cleared = sem("cleared" + name)
                    staged = sem("staged" + name)
                    landed = [sem(f"landed{name}{u}") for u in range(RING)]
                    matched = sem("matched" + name)
                    summed = sem("summed" + name)
                    added = sem("added" + name)
                    block = scope.enter_context(nc.Block())

                    @block.sync
                    def _(sp):
                        if way == 0:
                            sp.dma_start(slots_sb_b[:, :, :], slots_b.ap().rearrange("(p t) w -> p t w", t=T)).then_inc(slots_landed, 16)
                            sp.dma_start(owner_sb[0][:, :], owner_b.ap().rearrange("(a t) -> a t", a=1)).then_inc(slots_landed, 16)
                            sp.dma_start(slots_sb_f[:, :, :], slots_f.ap().rearrange("(p t) w -> p t w", t=T)).then_inc(slots_landed, 16)
                            sp.dma_start(owner_sb[1][:, :], owner_f.ap().rearrange("(a t) -> a t", a=1)).then_inc(slots_landed, 16)

                    @block.scalar
                    def _(act):
                        act.sem_inc(summed, RING)
                        act.wait_ge(slots_landed, 64)
                        with act.Fori(0, T // RING) as turn:
                            for q in range(RING // GROUP):
                                act.wait_ge(summed, turn * RING + (q + 1) * GROUP)
                                there, here = bass.ds(turn * RING + q * GROUP, GROUP), slice(q * GROUP, (q + 1) * GROUP)
                                act.activation(index[:, here], slots_sb[:, there, 0], ACT.Copy).then_inc(staged, 1)
                                act.activation(local[:, here], slots_sb[:, there, 1], ACT.Copy).then_inc(staged, 1)

                    @block.gpsimd
                    def _(pool):
                        with pool.Fori(0, T // RING) as turn:
                            for q in range(RING // GROUP):
                                pool.wait_ge(staged, turn * (2 * RING // GROUP) + 2 * (q + 1))
                                pool.nop(nofuse=True)
                                for u in range(q * GROUP, (q + 1) * GROUP):
                                    pool.indirect_dma_start(
                                        gathered[:, u, 0:D], None, table,
                                        bass.IndirectOffsetOnAxis(ap=index[:, u:u + 1], axis=0)).then_inc(landed[u], 16)
                        for u in range(RING):
                            pool.wait_ge(landed[u], T // RING * 16)

                    @block.vector
                    def _(dve):
                        dve.memset(acc[:, :], 0.0).then_inc(cleared, 1)
                        dve.memset(gathered[:, :, COUNT], 1.0).then_inc(cleared, 1)
                        dve.wait_ge(cleared, 2)
                        dve.wait_ge(slots_landed, 64)
                        dve.sem_inc(added, BANKS)

                        def add(turn, u):
                            at = dve.value_load(owner_sb[way][0:1, bass.ds(turn * RING + u, 1)], min_val=0, max_val=(NT - 1) * ROW)
                            dve.wait_ge(added, turn * RING + (u + BANKS))
                            dve.wait_ge(summed, turn * RING + (u + 1 + RING))
                            dve.tensor_tensor(acc[:, bass.ds(at, COUNT + 1)], acc[:, bass.ds(at, COUNT + 1)],
                                              ps_sum[:, u % BANKS, 0:COUNT + 1], ALU.add).then_inc(added, 1)

                        with dve.Fori(0, T // RING) as turn:
                            for u in range(RING):
                                if u % GROUP == 0:
                                    dve.wait_ge(staged, turn * (2 * RING // GROUP) + 2 * (u // GROUP + 1))
                                dve.tensor_scalar(match[:, u, :], iota[:, :], local[:, u:u + 1], None,
                                                  ALU.is_equal).then_inc(matched, 1)
                                if u >= 2:
                                    add(turn, u - 2)
                            add(turn, RING - 2)
                            add(turn, RING - 1)

                    @block.tensor
                    def _(pe):
                        pe.wait_ge(cleared, 2)
                        with pe.Fori(0, T // RING) as turn:
                            for u in range(RING):
                                pe.wait_ge(landed[u], turn * 16 + 16)
                                pe.wait_ge(added, turn * RING + (u + 1))
                                pe.wait_ge(matched, turn * RING + (u + 1))
                                nc.tensor.matmul(ps_sum[:, u % BANKS, 0:COUNT + 1], match[:, u, :],
                                                 gathered[:, u, 0:COUNT + 1], start=True, stop=True).then_inc(summed, 1)

            add_messages(0, slots_sb_b, table_b.ap().rearrange("n (r d) -> (n r) d", d=D), acc_b)
            add_messages(1, slots_sb_f, table_f.ap().rearrange("n (r d) -> (n r) d", d=D), acc_f)

            with ExitStack() as three:
                def s3(name, shape, dt=F32):
                    return sb(name, shape, dt, three)

                x_rows = s3("x_rows", [P, D])
                x_cols = s3("x_cols", [P, KC, P])
                w_loop = s3("w_loop", [P, KC, D])
                bias = [s3("bias_b", [P, D]), s3("bias_f", [P, D]), s3("bias_s", [P, D])]
                w_att = s3("w_att", [P, KC, D])
                a_att = s3("a_att", [P, KC, 2])
                w_z = s3("w_z", [P, KC, D + 2])
                inv = [s3("inv_b", [P, NT]), s3("inv_f", [P, NT])]
                some = [s3("some_b", [P, NT]), s3("some_f", [P, NT])]
                h = s3("h", [P, D])
                fresh = s3("fresh", [P, ROW])
                stats = s3("stats", [P, 6])
                moments = s3("moments", [P, 2])
                eps = s3("eps", [P, 1])
                spread = s3("spread", [P, 1])
                x1 = s3("x1", [P, D])
                x1T = s3("x1T", [P, KC, P])
                z_row = s3("z_row", [P, DENOM + 1])
                ps_loop = psum("ps_loop", [P, 512], three)[:, 0:D]
                ps_u = psum("ps_u", [P, 512], three)[:, 0:2 * KC].rearrange("p (k j) -> p k j", j=2)
                ps_t = psum("ps_t", [P, 512], three)[:, 0:D].rearrange("p (k n) -> p k n", n=P)
                ps_z = psum("ps_z", [P, 512], three)[:, 0:D + 2]
                weights_landed = sem("weights_landed")
                x_landed = sem("x_landed")
                vnorm = sem("vnorm")
                u_summed = sem("u_summed")
                looped = sem("looped")
                std_made = sem("std_made")
                x1_made = sem("x1_made")
                x1_turned = sem("x1_turned")
                x1T_made = sem("x1T_made")
                z_summed = sem("z_summed")
                z_made = sem("z_made")
                z_stored = sem("z_stored")
                block = three.enter_context(nc.Block())
                STEPS = 12
                PRE = 12

                @block.sync
                def _(sp):
                    for k in range(KC):
                        rows = slice(k * P, (k + 1) * P)
                        sp.dma_start(w_loop[:, k, :], loop_weight[rows, :]).then_inc(weights_landed, 16)
                        sp.dma_start(w_att[:, k, :], W1[rows, :]).then_inc(weights_landed, 16)
                        sp.dma_start(w_z[:, k, 0:D], W1T[rows, :]).then_inc(weights_landed, 16)
                        for j in range(2):
                            sp.dma_start(a_att[:, k, j:j + 1], A1[0:1, j * D + k * P:j * D + (k + 1) * P].rearrange("a p -> p a"))\
                                .then_inc(weights_landed, 16)
                    for b, vec in zip(bias, (backward_bias, forward_bias, self_bias)):
                        sp.dma_start(b[:, :], vec.rearrange("(a n) -> a n", a=1).to_broadcast([P, D])).then_inc(weights_landed, 16)

                    def load(t):
                        sp.dma_start(x_rows[:, :], x_pad[bass.ds(t * P, P), :]).then_inc(x_landed, 16)
                        sp.dma_start(x_cols[:, :, :], xT_pad[:, bass.ds(t * P, P)].rearrange("(k p) n -> p k n", p=P))\
                            .then_inc(x_landed, 16)

                    load(0)
                    with sp.Fori(0, NT - 1) as t:
                        sp.wait_ge(x1_made, t + 1)
                        load(t + 1)
                        sp.wait_ge(z_made, t * 2 + 2)
                        sp.dma_start(z_table.ap()[bass.ds(t * P, P), :], z_row[:, :]).then_inc(z_stored, 16)
                    sp.wait_ge(z_made, NT * 2)
                    sp.dma_start(z_table.ap()[(NT - 1) * P:NT * P, :], z_row[:, :]).then_inc(z_stored, 16)
                    sp.wait_ge(z_stored, NT * 16)

                @block.tensor
                def _(pe):
                    pe.wait_ge(weights_landed, 16 * (5 * KC + 3))
                    for k in range(KC):
                        for j in range(KC):
                            last = nc.tensor.matmul(ps_u[:, k, :], w_att[:, j, k * P:(k + 1) * P], a_att[:, j, :],
                                                    start=(j == 0), stop=(j == KC - 1))
                    last.then_inc(u_summed, 1)
                    with pe.Fori(0, NT) as t:
                        pe.wait_ge(x_landed, t * 32 + 32)
                        for k in range(KC):
                            last = nc.tensor.matmul(ps_loop[:, :], x_cols[:, k, :], w_loop[:, k, :],
                                                    start=(k == 0), stop=(k == KC - 1))
                        last.then_inc(looped, 1)
                        pe.wait_ge(x1_made, t + 1)
                        for k in range(KC):
                            last = nc.tensor.transpose(ps_t[:, k, :], x1[:, k * P:(k + 1) * P], ident[:, :])
                        last.then_inc(x1_turned, 1)
                        pe.wait_ge(x1T_made, t + 1)
                        for k in range(KC):
                            last = nc.tensor.matmul(ps_z[:, :], x1T[:, k, :], w_z[:, k, :],
                                                    start=(k == 0), stop=(k == KC - 1))
                        last.then_inc(z_summed, 1)

                @block.scalar
                def _(act):
                    def tile(t, first):
                        act.wait_ge(vnorm, t * STEPS + (PRE + 9))
                        act.activation(spread[:, :], moments[:, 1:2], ACT.Sqrt, bias=eps[:, 0:1]).then_inc(std_made, 1)
                        act.wait_ge(x1_turned, t + 1)
                        act.activation(x1T[:, :, :], ps_t[:, :, :], ACT.Copy).then_inc(x1T_made, 1)
                        if not first:
                            act.wait_ge(z_stored, t * 16)
                        act.wait_ge(z_summed, t + 1)
                        act.activation(z_row[:, 0:COUNT + 1], ps_z[:, 0:COUNT + 1], ACT.Copy).then_inc(z_made, 1)

                    tile(0, True)
                    with act.Fori(1, NT) as t:
                        tile(t, False)

                @block.vector
                def _(dve):
                    v = Tally(vnorm)
                    v.up(dve.memset(eps[:, :], EPS))
                    v.up(dve.memset(z_row[:, DENOM:DENOM + 1], 1.0))
                    for way, rows in ((0, rows_b), (1, rows_f)):
                        v.up(dve.tensor_scalar(inv[way][:, :], rows[:, :, COUNT], 1.0, None, ALU.max))
                        dve.wait_ge(vnorm, v.n)
                        v.up(dve.reciprocal(inv[way][:, :], inv[way][:, :]))
                        v.up(dve.tensor_scalar(some[way][:, :], rows[:, :, COUNT], 1.0, None, ALU.min))
                    dve.wait_ge(weights_landed, 16 * (5 * KC + 3))
                    dve.wait_ge(u_summed, 1)
                    for k in range(KC):
                        v.up(dve.tensor_copy(w_z[:, k, D:D + 2], ps_u[:, k, :]))
                    v.up(dve.memset(fresh[:, 0:NEG_MAX], 0.0))
                    v.up(dve.memset(fresh[:, NEG_MAX:ROW], FLOOR))
                    n = v.n
                    assert n == PRE
                    with dve.Fori(0, NT) as t:
                        at = t * ROW
                        sums_b, sums_f = acc_b[:, bass.ds(at, D)], acc_f[:, bass.ds(at, D)]

                        def step(k):
                            dve.wait_ge(vnorm, t * STEPS + (n + k))

                        dve.wait_ge(x_landed, t * 32 + 32)
                        step(0)
                        dve.scalar_tensor_tensor(h[:, :], sums_f, inv[1][:, bass.ds(t, 1)], x_rows[:, :], ALU.mult, ALU.add).then_inc(vnorm, 1)
                        step(1)
                        dve.scalar_tensor_tensor(h[:, :], sums_b, inv[0][:, bass.ds(t, 1)], h[:, :], ALU.mult, ALU.add).then_inc(vnorm, 1)
                        dve.wait_ge(looped, t + 1)
                        step(2)
                        dve.scalar_tensor_tensor(h[:, :], ps_loop[:, :], 2.0, h[:, :], ALU.mult, ALU.add).then_inc(vnorm, 1)
                        for k, way in ((3, 0), (4, 1)):
                            step(k)
                            dve.scalar_tensor_tensor(h[:, :], bias[way][:, :], some[way][:, bass.ds(t, 1)], h[:, :],
                                                     ALU.mult, ALU.add).then_inc(vnorm, 1)
                        step(5)
                        dve.tensor_tensor(h[:, :], h[:, :], bias[2][:, :], ALU.add).then_inc(vnorm, 1)
                        step(6)
                        dve.bn_stats(stats[:, :], h[:, :]).then_inc(vnorm, 1)
                        step(7)
                        dve.nop(nofuse=True)
                        dve.bn_aggr(moments[:, :], stats[:, :]).then_inc(vnorm, 1)
                        step(8)
                        dve.tensor_scalar(acc_b[:, bass.ds(at, NEG_MAX)], fresh[:, 0:NEG_MAX], 1.0, None, ALU.mult).then_inc(vnorm, 1)
                        dve.wait_ge(std_made, t + 1)
                        step(9)
                        dve.reciprocal(spread[:, :], spread[:, :]).then_inc(vnorm, 1)
                        step(10)
                        dve.tensor_scalar(x1[:, :], h[:, :], moments[:, 0:1], spread[:, 0:1], ALU.subtract, ALU.mult)\
                            .then_inc(vnorm, 1)
                        step(11)
                        dve.tensor_scalar(acc_f[:, bass.ds(at, D)], x1[:, :], 1.0, None, ALU.mult).then_inc(x1_made, 1)
                        dve.tensor_scalar(acc_b[:, bass.ds(at + NEG_MAX, 1)], fresh[:, NEG_MAX:ROW - 1], 1.0, None, ALU.mult)\
                            .then_inc(vnorm, 1)
                        dve.wait_ge(z_made, t * 2 + 1)
                        dve.tensor_scalar(acc_b[:, bass.ds(at + S_DST, 1)], ps_z[:, D + 1:D + 2], 1.0, None, ALU.mult)\
                            .then_inc(z_made, 1)

            with ExitStack() as four:
                def s4(name, shape, dt=F32):
                    return sb(name, shape, dt, four)

                spread_e = s4("spread_e", [P, RING, P])
                logit = s4("logit", [P, RING, P])
                prob = s4("prob", [P, RING, P])
                probT = s4("probT", [P, RING, P])
                v_edge = s4("v_edge", [P, RING])
                s_dst = s4("s_dst", [P, RING])
                top = s4("top", [P, RING])
                neg_max = s4("neg_max", [P, RING])
                drop = s4("drop", [P, RING])
                shrink = s4("shrink", [P, RING])
                ps_v = psum("ps_v", [P, 2, 512], four)
                ps_p = psum("ps_p", [P, 2, 512], four)
                ps_o = psum("ps_o", [P, BANKS, 512], four)
                staged = sem("staged_a")
                landed = [sem(f"landed_a{u}") for u in range(RING)]
                masked = sem("masked")
                v_made = sem("v_made")
                spread_made = sem("spread_made")
                v_turned = sem("v_turned")
                logit_made = sem("logit_made")
                maxed = sem("maxed")
                prob_made = sem("prob_made")
                prob_turned = sem("prob_turned")
                probT_made = sem("probT_made")
                summed = sem("summed_a")
                added = sem("added_a")
                block = four.enter_context(nc.Block())

                def staggered(eng, stages):
                    for u in range(RING):
                        for stage, lag in stages:
                            if u >= lag:
                                stage(0, u - lag, u - lag)
                    with eng.Fori(1, T // RING) as turn:
                        for u in range(RING):
                            for stage, lag in stages:
                                stage(turn, u - lag, (u - lag) % RING)
                    for u in range(max(lag for _, lag in stages)):
                        for stage, lag in stages:
                            if u < lag:
                                stage(T // RING, u - lag, (u - lag) % RING)

                @block.gpsimd
                def _(pool):
                    with pool.Fori(0, T // RING) as turn:
                        for q in range(RING // GROUP):
                            pool.wait_ge(staged, turn * (3 * RING // GROUP) + 3 * (q + 1))
                            pool.nop(nofuse=True)
                            for u in range(q * GROUP, (q + 1) * GROUP):
                                pool.indirect_dma_start(
                                    gathered[:, u, 0:DENOM + 1], None, z_table.ap(),
                                    bass.IndirectOffsetOnAxis(ap=index[:, u:u + 1], axis=0)).then_inc(landed[u], 16)
                    for u in range(RING):
                        pool.wait_ge(landed[u], T // RING * 16)

                @block.scalar
                def _(act):
                    act.sem_inc(summed, RING)

                    def stage(turn, du, u):
                        if u % GROUP:
                            return
                        act.wait_ge(summed, turn * RING + (du + GROUP))
                        there, here = bass.ds(turn * RING + du, GROUP), slice(u, u + GROUP)
                        act.activation(index[:, here], slots_sb_f[:, there, 2], ACT.Copy).then_inc(staged, 1)
                        act.activation(local[:, here], slots_sb_f[:, there, 1], ACT.Copy).then_inc(staged, 1)
                        act.activation(dot_e[:, here], slots_sb_f[:, there, 3], ACT.Copy).then_inc(staged, 1)

                    def add_v(turn, du, u):
                        act.wait_ge(v_made, turn * (2 * RING) + (2 * du + 2))
                        act.activation(spread_e[:, u, :], spread_e[:, u, :], ACT.Identity, bias=v_edge[:, u:u + 1])\
                            .then_inc(spread_made, 1)

                    def to_logit(turn, du, u):
                        act.wait_ge(v_turned, turn * RING + (du + 1))
                        act.activation(logit[:, u, :], ps_v[:, u % 2, 0:P], ACT.Identity, bias=s_dst[:, u:u + 1])\
                            .then_inc(logit_made, 1)

                    def to_prob(turn, du, u):
                        act.wait_ge(maxed, turn * (5 * RING) + (5 * du + 5))
                        act.activation(prob[:, u, :], logit[:, u, :], ACT.Exp, bias=neg_max[:, u:u + 1]).then_inc(prob_made, 1)
                        act.activation(shrink[:, u:u + 1], drop[:, u:u + 1], ACT.Exp).then_inc(prob_made, 1)

                    def copy_probT(turn, du, u):
                        act.wait_ge(prob_turned, turn * RING + (du + 1))
                        act.activation(probT[:, u, :], ps_p[:, u % 2, 0:P], ACT.Copy).then_inc(probT_made, 1)

                    staggered(act, [(stage, 0), (add_v, 5), (to_logit, 6), (to_prob, 7), (copy_probT, 8)])

                @block.vector
                def _(dve):
                    dve.sem_inc(added, BANKS)

                    def owner_of(turn, du):
                        return dve.value_load(owner_sb[1][0:1, bass.ds(turn * RING + du, 1)], min_val=0, max_val=(NT - 1) * ROW)

                    def mask(turn, du, u):
                        if u % GROUP == 0:
                            dve.wait_ge(staged, turn * (3 * RING // GROUP) + (3 * (du // GROUP) + 3))
                        dve.tensor_scalar(spread_e[:, u, :], iota[:, :], local[:, u:u + 1], -FAR, ALU.not_equal, ALU.mult)\
                            .then_inc(masked, 1)

                    def make_v(turn, du, u):
                        at = owner_of(turn, du)
                        dve.tensor_copy(s_dst[:, u:u + 1], acc_b[:, bass.ds(at + S_DST, 1)]).then_inc(v_made, 1)
                        dve.wait_ge(landed[u], turn * 16 + (16 if du >= 0 else 0))
                        dve.tensor_tensor(v_edge[:, u:u + 1], gathered[:, u, D:D + 1], dot_e[:, u:u + 1], ALU.add)\
                            .then_inc(v_made, 1)

                    def new_max(turn, du, u):
                        at = owner_of(turn, du)
                        old = acc_b[:, bass.ds(at + NEG_MAX, 1)]

                        def step(k):
                            dve.wait_ge(maxed, turn * (5 * RING) + (5 * du + k))

                        dve.wait_ge(logit_made, turn * RING + (du + 1))
                        dve.scalar_tensor_tensor(logit[:, u, :], logit[:, u, :], ALPHA, logit[:, u, :], ALU.mult, ALU.max)\
                            .then_inc(maxed, 1)
                        step(1)
                        dve.tensor_reduce(top[:, u:u + 1], logit[:, u, :], AX.X, ALU.max).then_inc(maxed, 1)
                        step(2)
                        dve.scalar_tensor_tensor(neg_max[:, u:u + 1], top[:, u:u + 1], -1.0, old, ALU.mult, ALU.min).then_inc(maxed, 1)
                        step(3)
                        dve.tensor_tensor(drop[:, u:u + 1], neg_max[:, u:u + 1], old, ALU.subtract).then_inc(maxed, 1)
                        step(4)
                        dve.tensor_scalar(old, neg_max[:, u:u + 1], 1.0, None, ALU.mult).then_inc(maxed, 1)

                    def add(turn, du, u):
                        at = owner_of(turn, du)
                        sums = acc_b[:, bass.ds(at, DENOM + 1)]
                        dve.wait_ge(added, turn * RING + (du + BANKS))
                        dve.wait_ge(summed, turn * RING + (du + 1 + RING))
                        dve.scalar_tensor_tensor(sums, sums, shrink[:, u:u + 1], ps_o[:, u % BANKS, 0:DENOM + 1],
                                                 ALU.mult, ALU.add).then_inc(added, 1)

                    staggered(dve, [(mask, 0), (make_v, 4), (new_max, 6), (add, 9)])

                @block.tensor
                def _(pe):
                    def turn_v(turn, du, u):
                        pe.wait_ge(spread_made, turn * RING + (du + 1))
                        nc.tensor.transpose(ps_v[:, u % 2, 0:P], spread_e[:, u, :], ident[:, :]).then_inc(v_turned, 1)

                    def turn_prob(turn, du, u):
                        pe.wait_ge(prob_made, turn * (2 * RING) + (2 * du + 2))
                        nc.tensor.transpose(ps_p[:, u % 2, 0:P], prob[:, u, :], ident[:, :]).then_inc(prob_turned, 1)

                    def sum_up(turn, du, u):
                        pe.wait_ge(added, turn * RING + (du + 1))
                        pe.wait_ge(probT_made, turn * RING + (du + 1))
                        nc.tensor.matmul(ps_o[:, u % BANKS, 0:DENOM + 1], probT[:, u, :], gathered[:, u, 0:DENOM + 1],
                                         start=True, stop=True).then_inc(summed, 1)

                    staggered(pe, [(turn_v, 5), (turn_prob, 7), (sum_up, 8)])

        with ExitStack() as five:
            h = sb("h2", [P, D], scope=five)
            stats = sb("stats2", [P, 6], scope=five)
            moments = sb("moments2", [P, 2], scope=five)
            eps = sb("eps2", [P, 1], scope=five)
            spread = sb("spread2", [P, 1], scope=five)
            inv = sb("inv2", [P, NT], scope=five)
            vlast = sem("vlast")
            std_made = sem("std2_made")
            out_stored = sem("out_stored")
            block = five.enter_context(nc.Block())

            @block.sync
            def _(sp):
                with sp.Fori(0, NT) as t:
                    sp.wait_ge(vlast, t * 5 + 8)
                    sp.dma_start(out[bass.ds(t * P, P), :], acc_f[:, bass.ds(t * ROW, D)]).then_inc(out_stored, 16)
                sp.wait_ge(out_stored, NT * 16)

            @block.scalar
            def _(act):
                with act.Fori(0, NT) as t:
                    act.wait_ge(vlast, t * 5 + 6)
                    act.activation(spread[:, :], moments[:, 1:2], ACT.Sqrt, bias=eps[:, 0:1]).then_inc(std_made, 1)

            @block.vector
            def _(dve):
                dve.memset(eps[:, :], EPS).then_inc(vlast, 1)
                dve.tensor_scalar(inv[:, :], rows_b[:, :, DENOM], 1e-30, None, ALU.max).then_inc(vlast, 1)
                dve.wait_ge(vlast, 2)
                dve.reciprocal(inv[:, :], inv[:, :]).then_inc(vlast, 1)
                with dve.Fori(0, NT) as t:
                    x1 = acc_f[:, bass.ds(t * ROW, D)]
                    dve.wait_ge(vlast, t * 5 + 3)
                    dve.scalar_tensor_tensor(h[:, :], acc_b[:, bass.ds(t * ROW, D)], inv[:, bass.ds(t, 1)], x1,
                                             ALU.mult, ALU.add).then_inc(vlast, 1)
                    dve.wait_ge(vlast, t * 5 + 4)
                    dve.bn_stats(stats[:, :], h[:, :]).then_inc(vlast, 1)
                    dve.wait_ge(vlast, t * 5 + 5)
                    dve.nop(nofuse=True)
                    dve.bn_aggr(moments[:, :], stats[:, :]).then_inc(vlast, 1)
                    dve.wait_ge(std_made, t + 1)
                    dve.reciprocal(spread[:, :], spread[:, :]).then_inc(vlast, 1)
                    dve.wait_ge(vlast, t * 5 + 7)
                    dve.tensor_scalar(x1, h[:, :], moments[:, 0:1], spread[:, 0:1], ALU.subtract, ALU.mult)\
                        .then_inc(vlast, 1)


_INS = ["x_pad", "xT_pad", "src", "dst", "edge_attr_64", "edge_type_16", "L0_gnn_Wf", "L0_gnn_Wb",
        "L0_gnn_loop_weight", "L0_gnn_forward_bias", "L0_gnn_backward_bias", "L0_gnn_self_bias",
        "L1_gnn_W", "L1_gnn_WT", "L1_gnn_A"]


def kernel(**inputs):
    import numpy as _np
    import concourse.bacc as _bacc
    from concourse import mybir as _mybir
    from concourse.bass_utils import run_bass_kernel_spmd as _run

    n, d = inputs["x"].shape
    n_pad = -(-n // 128) * 128
    x_pad = _np.zeros((n_pad, d), _np.float32)
    x_pad[:n] = inputs["x"]
    laid = dict(inputs)
    laid["x_pad"] = x_pad
    laid["xT_pad"] = x_pad.T
    laid["L1_gnn_WT"] = _np.asarray(inputs["L1_gnn_W"]).T

    nc = _bacc.Bacc("TRN2", target_bir_lowering=False, num_devices=1)
    arrays, args = {}, []
    for name in _INS:
        a = _np.ascontiguousarray(laid[name])
        arrays[f"in_{name}_dram"] = a
        args.append(nc.dram_tensor(f"in_{name}_dram", a.shape, _mybir.dt.from_np(a.dtype), kind="ExternalInput").ap())
    out = nc.dram_tensor("out_0_dram", (n_pad, d), _mybir.dt.float32, kind="ExternalOutput").ap()
    gnn(nc, *args, out)
    r = _run(nc, [arrays], core_ids=[0])
    return r.results[0]["out_0_dram"][:n]
```

```python
from contextlib import ExitStack

import concourse.bass as bass
from concourse import mybir

P = 128
F32 = mybir.dt.float32
I32 = mybir.dt.int32
U32 = mybir.dt.uint32
U16 = mybir.dt.uint16
ALU = mybir.AluOpType
ACT = mybir.ActivationFunctionType
AX = mybir.AxisListType

EDGE_ROWS = 125
HALF = 15
GROUP = 4
RING = 6
BANKS = 4
ROW = 260
COUNT = 256
DENOM = 257
NEG_MAX = 258
S_DST = 259
EPS = 1e-5
ALPHA = 0.2
FAR = 1e30
FLOOR = 1e28


class Tally:

    def __init__(self, sem):
        self.sem, self.n = sem, 0

    def up(self, instruction):
        instruction.then_inc(self.sem, 1)
        self.n += 1


def gnn(nc, x_pad, xT_pad, src, dst, edge_attr, edge_type, Wf, Wb, loop_weight, forward_bias,
        backward_bias, self_bias, W1, W1T, A1, out):
    NPAD, D = x_pad.shape
    E, ED = edge_attr.shape
    R = Wf.shape[0]
    KC = D // P
    NT = NPAD // P
    EC = E // EDGE_ROWS
    assert EC * EDGE_ROWS == E and EC % (2 * HALF) == 0 and D == 2 * P and R * D % 1024 == 0
    SIZE = GROUP * P
    LOG = SIZE.bit_length() - 1
    GROUPS = -(-((E + NT * (SIZE - 1)) // SIZE) // RING) * RING
    TURNS = GROUPS // RING
    GC = -(-GROUPS // P)
    T = GROUPS * GROUP
    BLANK = max(b for b in range(1, 65) if T % b == 0)
    SCATTER_STEPS = EC // (2 * HALF)
    EDGE_STEPS = max(2, SCATTER_STEPS // 5)
    CHUNK = EC // (2 * EDGE_STEPS)
    PAIRS = (NT - 1) // 2
    assert CHUNK * 2 * EDGE_STEPS == EC and PAIRS > 1 and BLANK >= GROUP
    HALF_W = R * D // 2
    BLOCKS = HALF_W // 512

    table_f = nc.dram_tensor("table_f", (NPAD, R * D), F32)
    table_b = nc.dram_tensor("table_b", (NPAD, R * D), F32)
    z_table = nc.dram_tensor("z_table", (NPAD, DENOM + 1), F32)
    slots_b = nc.dram_tensor("slots_b", (P * T, 2), F32)
    sorted_f = nc.dram_tensor("sorted_f", (E + SIZE, 4), F32)
    owner_b = nc.dram_tensor("owner_b", (P * GC,), I32)
    owner_f = nc.dram_tensor("owner_f", (P * GC,), I32)
    start_f = nc.dram_tensor("start_f", (P * GC,), I32)
    first_f = nc.dram_tensor("first_f", (P * GC,), F32)

    with ExitStack() as whole:
        def sem(name):
            return whole.enter_context(nc.semaphore(name))

        def sb(name, shape, dt=F32, scope=whole):
            return scope.enter_context(nc.sbuf_tensor(name, shape, dt))

        def psum(name, shape, scope):
            return scope.enter_context(nc.psum_tensor(name, shape, F32))

        iota = sb("iota", [P, P])
        iota_i = sb("iota_i", [P, P], I32)
        row_i = sb("row_i", [P, 1], I32)
        row_f = sb("row_f", [P, 1])
        ident = sb("ident", [P, P])

        with ExitStack() as one:
            def s1(name, shape, dt=F32):
                return sb(name, shape, dt, one)

            src_i = s1("src_i", [EDGE_ROWS, EC], I32)
            dst_i = s1("dst_i", [EDGE_ROWS, EC], I32)
            type_i = s1("type_i", [EDGE_ROWS, EC], I32)
            feat = s1("feat", [EDGE_ROWS, 2, CHUNK, ED])
            a_edge = s1("a_edge", [EDGE_ROWS, ED])
            work_i = s1("work_i", [EDGE_ROWS, EC], I32)
            bucket = s1("bucket", [EDGE_ROWS, EC])
            inside = s1("inside", [EDGE_ROWS, EC], U16)
            ranks = s1("ranks", [EDGE_ROWS, EC])
            place = s1("place", [EDGE_ROWS, EC])
            nil = s1("nil", [EDGE_ROWS, 1])
            edge_i = s1("edge_i", [EDGE_ROWS, EC], I32)
            astray = s1("astray", [EDGE_ROWS, 1])
            astray_i = s1("astray_i", [1, 1], I32)
            addr = [s1("addr_b", [EDGE_ROWS, EC], U32), s1("addr_f", [EDGE_ROWS, EC], U32)]
            recs = [s1("recs_b", [EDGE_ROWS, EC, 2]), s1("recs_f", [EDGE_ROWS, EC, 4])]
            below = s1("below", [EDGE_ROWS, P])
            ones = s1("ones", [EDGE_ROWS, P])
            group_i = s1("group_i", [P, GC], I32)
            group_f = s1("group_f", [P, GC])
            count = s1("count", [EDGE_ROWS, NT])
            groups_i = s1("groups_i", [P, NT], I32)
            groups = s1("groups", [P, NT])
            tend = s1("tend", [P, NT])
            base = s1("base", [P, NT])
            past = s1("past", [P, GC, NT])
            owner = s1("owner", [P, GC])
            owner_i = [s1("owner_ib", [P, GC], I32), s1("owner_if", [P, GC], I32)]
            spare = s1("spare", [P, NT])
            start = s1("start", [P, GC])
            start_i = s1("start_i", [P, GC], I32)
            first = s1("first", [P, GC])
            blank_b = s1("blank_b", [P, BLANK, 2])
            blank_f = s1("blank_f", [P, BLANK, 4])
            w_rel = s1("w_rel", [P, KC, R, D])
            xT = s1("xT", [P, 2, KC, P])
            proj = s1("proj", [P, 2, HALF_W])
            stage_rec = [s1("stage_recb", [EDGE_ROWS, 2, HALF, 2]), s1("stage_recf", [EDGE_ROWS, 2, HALF, 4])]
            stage_addr = s1("stage_addr", [EDGE_ROWS, 2, HALF], U32)
            ps_proj = psum("ps_proj", [P, BANKS, 512], one)
            ps_count = psum("ps_count", [P, 512], one)[:, 0:4 * NT].rearrange("p (w k t) -> p w k t", w=2, k=2)
            ps_astray = psum("ps_astray", [P, 512], one)[:, 0:1]

            keys_landed = sem("keys_landed")
            type_landed = sem("type_landed")
            a_edge_landed = sem("a_edge_landed")
            feat_landed = [sem("feat_landed0"), sem("feat_landed1")]
            feat_used = sem("feat_used")
            iotas = sem("iotas")
            blanks = sem("blanks")
            blank_stored = sem("blank_stored")
            vdone = sem("vdone")
            counted = [sem("counted_b"), sem("counted_f")]
            count_summed = [sem("count_summed_b"), sem("count_summed_f")]
            astray_found = sem("astray_found")
            astray_summed = sem("astray_summed")
            astray_known = sem("astray_known")
            tail_stored = sem("tail_stored")
            edges_stored = sem("edges_stored")
            owner_made = sem("owner_made")
            owner_stored = sem("owner_stored")
            placed = [sem("placed_b"), sem("placed_f")]
            features_dotted = sem("features_dotted")
            staged = [sem("scatter_staged0"), sem("scatter_staged1")]
            scattered = [sem("scattered0"), sem("scattered1")]
            w_landed = sem("w_landed")
            xT_landed = [sem("xT_landed0"), sem("xT_landed1")]
            proj_summed = sem("proj_summed")
            proj_copied = sem("proj_copied")
            proj_stored = [sem("proj_stored0"), sem("proj_stored1")]

            block = one.enter_context(nc.Block())

            @block.sync
            def _(sp):
                sp.dma_start(src_i[:, :], src.rearrange("(p c) -> p c", c=EC)).then_inc(keys_landed, 16)
                sp.dma_start(dst_i[:, :], dst.rearrange("(p c) -> p c", c=EC)).then_inc(keys_landed, 16)
                sp.dma_start(type_i[:, :], edge_type.rearrange("(p c) -> p c", c=EC)).then_inc(type_landed, 16)
                sp.dma_start(a_edge[:, :], A1[:, 2 * D:].to_broadcast([EDGE_ROWS, ED])).then_inc(a_edge_landed, 16)
                sp.wait_ge(blanks, 4)
                blank_rows_b = slots_b.ap().rearrange("(p t) w -> p t w", t=T)
                for c in range(T // BLANK):
                    here = slice(c * BLANK, (c + 1) * BLANK)
                    sp.dma_start(blank_rows_b[:, here, :], blank_b[:, :, :]).then_inc(blank_stored, 16)

                sp.dma_start(sorted_f.ap()[E:E + SIZE, :].rearrange("(p u) w -> p u w", u=GROUP), blank_f[:, 0:GROUP, :])\
                    .then_inc(tail_stored, 16)

                feat_rows = edge_attr.rearrange("(p c) f -> p c f", c=EC)

                def load_features(step, half):
                    sp.dma_start(feat[:, half, :, :], feat_rows[:, bass.ds(step * 2 * CHUNK + half * CHUNK, CHUNK), :])\
                        .then_inc(feat_landed[half], 16)

                def stage(way, step, half):
                    c0 = step * 2 * HALF + half * HALF
                    sp.dma_start(stage_rec[way][:, half, :, :], recs[way][:, bass.ds(c0, HALF), :]).then_inc(staged[half], 16)
                    sp.dma_start(stage_addr[:, half, :], addr[way][:, bass.ds(c0, HALF)]).then_inc(staged[half], 16)

                load_features(0, 0)
                load_features(0, 1)
                sp.wait_ge(placed[0], 1)
                stage(0, 0, 0)
                stage(0, 0, 1)
                with sp.Fori(1, EDGE_STEPS) as step:
                    for half in range(2):
                        sp.wait_ge(scattered[half], step * 16 * HALF)
                        stage(0, step, half)
                    for half in range(2):
                        sp.wait_ge(feat_used, step * 2 + (half - 1))
                        load_features(step, half)
                with sp.Fori(EDGE_STEPS, SCATTER_STEPS) as step:
                    for half in range(2):
                        sp.wait_ge(scattered[half], step * 16 * HALF)
                        stage(0, step, half)
                sp.wait_ge(placed[1], 1)
                sp.wait_ge(features_dotted, 1)
                sp.wait_ge(astray_known, 1)
                moved = sp.alloc_register("moved_sp")
                sp.reg_load(moved, astray_i[0:1, 0:1])
                with sp.If_ne(moved, 0):
                    with sp.Fori(0, SCATTER_STEPS) as step:
                        for half in range(2):
                            sp.wait_ge(scattered[half], (step + SCATTER_STEPS) * 16 * HALF)
                            stage(1, step, half)
                with sp.Else():
                    sp.dma_start(sorted_f.ap()[0:E, :].rearrange("(p c) w -> p c w", c=EC), recs[1][:, :, :])\
                        .then_inc(edges_stored, 16)
                    sp.wait_ge(edges_stored, 16)
                sp.wait_ge(tail_stored, 16)
                sp.wait_ge(owner_stored, 64)

            @block.gpsimd
            def _(pool):
                pool.iota(iota_i[:, :], pattern=[[1, P]], base=0, channel_multiplier=0).then_inc(iotas, 1)
                pool.iota(row_i[:, :], pattern=[[0, 1]], base=0, channel_multiplier=1).then_inc(iotas, 1)
                pool.iota(group_i[:, :], pattern=[[1, GC]], base=0, channel_multiplier=GC).then_inc(iotas, 1)
                pool.iota(edge_i[:, :], pattern=[[1, EC]], base=1, channel_multiplier=EC).then_inc(iotas, 1)
                pool.memset(blank_b[:, :, 0], 0.0).then_inc(blanks, 1)
                pool.memset(blank_b[:, :, 1], -1.0).then_inc(blanks, 1)
                pool.memset(blank_f[:, :, 0:4], 0.0).then_inc(blanks, 1)
                pool.wait_ge(blanks, 3)
                pool.memset(blank_f[:, :, 1], -1.0).then_inc(blanks, 1)
                pool.wait_ge(blank_stored, 16 * (T // BLANK))

                def scatter_all(way, slots):
                    def scatter(half):
                        for c in range(HALF):
                            pool.indirect_dma_start(
                                slots.ap(), bass.IndirectOffsetOnAxis(ap=stage_addr[:, half, c:c + 1], axis=0),
                                stage_rec[way][:, half, c, :], None).then_inc(scattered[half], 16)

                    with pool.Fori(0, SCATTER_STEPS) as step:
                        for half in range(2):
                            pool.wait_ge(staged[half], step * 32 + (way * SCATTER_STEPS + 1) * 32)
                            pool.nop(nofuse=True)
                            scatter(half)
                    for half in range(2):
                        pool.wait_ge(scattered[half], (way + 1) * SCATTER_STEPS * HALF * 16)

                scatter_all(0, slots_b)
                pool.wait_ge(astray_known, 1)
                moved = pool.alloc_register("moved_pool")
                pool.reg_load(moved, astray_i[0:1, 0:1])
                with pool.If_ne(moved, 0):
                    scatter_all(1, sorted_f)

            @block.vector
            def _(dve):
                v = Tally(vdone)
                dve.wait_ge(iotas, 4)
                v.up(dve.tensor_copy(iota[:, :], iota_i[:, :]))
                v.up(dve.tensor_copy(row_f[:, :], row_i[:, :]))
                v.up(dve.tensor_copy(group_f[:, :], group_i[:, :]))
                v.up(dve.memset(ones[:, :], 1.0))
                v.up(dve.memset(nil[:, :], 0.0))
                dve.wait_ge(vdone, v.n)
                v.up(dve.tensor_scalar(ident[:, :], iota[:, :], row_f[:, 0:1], None, ALU.is_equal))
                v.up(dve.tensor_scalar(below[:, :], iota[0:EDGE_ROWS, :], row_f[0:EDGE_ROWS, 0:1], None, ALU.is_gt))
                dve.wait_ge(keys_landed, 32)
                for way, key, other in ((0, src_i, dst_i), (1, dst_i, src_i)):
                    dve.wait_ge(vdone, v.n)
                    v.up(dve.tensor_scalar(work_i[:, :], key[:, :], 7, None, ALU.logical_shift_right))
                    dve.wait_ge(vdone, v.n)
                    v.up(dve.tensor_copy(bucket[:, :], work_i[:, :]))
                    if way == 0:
                        dve.wait_ge(vdone, v.n)
                        v.up(dve.tensor_scalar(work_i[:, :], key[:, :], P - 1, None, ALU.bitwise_and))
                        dve.wait_ge(vdone, v.n)
                        v.up(dve.tensor_copy(recs[way][:, :, 1], work_i[:, :]))
                    else:
                        v.up(dve.tensor_copy(recs[way][:, :, 1], key[:, :]))
                    n = v.n
                    with dve.Fori(0, NT) as b:
                        dve.wait_ge(vdone, b + n)
                        dve.tensor_scalar(inside[:, :], bucket[:, :], iota[0:EDGE_ROWS, bass.ds(b, 1)], None,
                                          ALU.is_equal, ALU.add, accum_out=count[:, bass.ds(b, 1)]).then_inc(vdone, 1)
                    v.n += NT
                    dve.wait_ge(vdone, v.n)
                    dve.sem_inc(counted[way], 1)
                    dve.wait_ge(count_summed[way], 1)
                    v.up(dve.tensor_scalar(groups[:, :], ps_count[:, way, 0, :], float(SIZE - 1), None, ALU.add))
                    dve.wait_ge(vdone, v.n)
                    v.up(dve.tensor_copy(groups_i[:, :], groups[:, :]))
                    dve.wait_ge(vdone, v.n)
                    v.up(dve.tensor_scalar(groups_i[:, :], groups_i[:, :], LOG, None, ALU.logical_shift_right))
                    dve.wait_ge(vdone, v.n)
                    v.up(dve.tensor_copy(groups[:, :], groups_i[:, :]))
                    dve.wait_ge(vdone, v.n)
                    v.up(dve.memset(base[:, :], 0.0))
                    v.up(dve.memset(place[:, :], 1.0))
                    dve.wait_ge(vdone, v.n)
                    v.up(dve.tensor_tensor_scan(tend[:, :], groups[:, :], base[:, :], 0.0, ALU.add, ALU.add))
                    dve.wait_ge(vdone, v.n)
                    v.up(dve.tensor_sub(base[:, :], tend[:, :], groups[:, :]))
                    dve.wait_ge(vdone, v.n)
                    if way == 0:
                        v.up(dve.scalar_tensor_tensor(base[:, :], base[:, :], float(SIZE), ps_count[:, way, 1, :], ALU.mult, ALU.add))
                    else:
                        v.up(dve.scalar_tensor_tensor(spare[:, :], groups[:, :], -float(SIZE), ps_count[:, way, 0, :], ALU.mult, ALU.add))
                        dve.wait_ge(vdone, v.n)
                        v.up(dve.tensor_scalar(groups[:, :], ps_count[:, way, 0, :], 1.0, None, ALU.mult))
                        v.up(dve.memset(base[:, :], 0.0))
                        dve.wait_ge(vdone, v.n)
                        v.up(dve.tensor_tensor_scan(base[:, :], groups[:, :], base[:, :], 0.0, ALU.add, ALU.add))
                        dve.wait_ge(vdone, v.n)
                        v.up(dve.tensor_sub(base[:, :], base[:, :], groups[:, :]))
                        dve.wait_ge(vdone, v.n)
                        v.up(dve.tensor_tensor(base[:, :], base[:, :], ps_count[:, way, 1, :], ALU.add))
                    n = v.n
                    with dve.Fori(0, NT) as b:
                        dve.wait_ge(vdone, b * 3 + n)
                        dve.tensor_scalar(inside[:, :], bucket[:, :], iota[0:EDGE_ROWS, bass.ds(b, 1)], None,
                                          ALU.is_equal).then_inc(vdone, 1)
                        dve.wait_ge(vdone, b * 3 + (n + 1))
                        dve.tensor_tensor_scan(ranks[:, :], inside[:, :], nil[:, 0:1].to_broadcast([EDGE_ROWS, EC]), base[0:EDGE_ROWS, bass.ds(b, 1)],
                                               ALU.add, ALU.add).then_inc(vdone, 1)
                        dve.wait_ge(vdone, b * 3 + (n + 2))
                        dve.nop(nofuse=True)
                        dve.copy_predicated(place[:, :], inside[:, :], ranks[:, :]).then_inc(vdone, 1)
                    v.n += 3 * NT
                    dve.wait_ge(vdone, v.n)
                    if way == 0:
                        v.up(dve.tensor_scalar(work_i[:, :], place[:, :], -1.0, None, ALU.add))
                        dve.wait_ge(vdone, v.n)
                        v.up(dve.tensor_scalar(ranks[:, :].bitcast(I32), work_i[:, :], P - 1, None, ALU.bitwise_and))
                        v.up(dve.tensor_scalar(place[:, :].bitcast(I32), work_i[:, :], 7, None, ALU.logical_shift_right))
                        dve.wait_ge(vdone, v.n)
                        v.up(dve.scalar_tensor_tensor(addr[way][:, :], ranks[:, :].bitcast(I32), float(T), place[:, :].bitcast(I32),
                                                      ALU.mult, ALU.add))
                    else:
                        v.up(dve.tensor_scalar(addr[way][:, :], place[:, :], -1.0, None, ALU.add))
                        v.up(dve.tensor_tensor(ranks[:, :], place[:, :], edge_i[:, :], ALU.not_equal))
                        dve.wait_ge(vdone, v.n)
                        v.up(dve.tensor_reduce(astray[:, :], ranks[:, :], AX.X, ALU.add))
                        dve.wait_ge(vdone, v.n)
                        dve.sem_inc(astray_found, 1)
                    if way == 0:
                        dve.wait_ge(type_landed, 16)
                    v.up(dve.scalar_tensor_tensor(recs[way][:, :, 0], other[:, :], float(R), type_i[:, :], ALU.mult, ALU.add))
                    if way == 1:
                        v.up(dve.tensor_copy(recs[way][:, :, 2], other[:, :]))
                    dve.wait_ge(vdone, v.n)
                    dve.sem_inc(placed[way], 1)
                    v.up(dve.tensor_tensor(past[:, :, :], group_f[:, :].unsqueeze(2).to_broadcast([P, GC, NT]),
                                           tend[:, :].unsqueeze(1).to_broadcast([P, GC, NT]), ALU.is_ge))
                    dve.wait_ge(vdone, v.n)
                    v.up(dve.tensor_reduce(owner[:, :], past[:, :, :], AX.X, ALU.add))
                    dve.wait_ge(vdone, v.n)
                    v.up(dve.tensor_scalar(owner_i[way][:, :], owner[:, :], float(NT - 1), float(ROW), ALU.min, ALU.mult))
                    if way == 1:
                        v.up(dve.tensor_scalar(first[:, :], owner[:, :], float(NT - 1), float(P), ALU.min, ALU.mult))
                        v.up(dve.tensor_tensor(past[:, :, :], past[:, :, :], spare[:, :].unsqueeze(1).to_broadcast([P, GC, NT]), ALU.mult))
                        dve.wait_ge(vdone, v.n)
                        v.up(dve.tensor_reduce(start[:, :], past[:, :, :], AX.X, ALU.add))
                        dve.wait_ge(vdone, v.n)
                        v.up(dve.scalar_tensor_tensor(start[:, :], group_f[:, :], float(SIZE), start[:, :], ALU.mult, ALU.add))
                        dve.wait_ge(vdone, v.n)
                        v.up(dve.tensor_scalar(start_i[:, :], start[:, :], float(E), None, ALU.min))
                        dve.wait_ge(astray_summed, 1)
                        dve.tensor_copy(astray_i[:, :], ps_astray[0:1, :]).then_inc(astray_known, 1)
                    dve.wait_ge(vdone, v.n)
                    dve.sem_inc(owner_made, 1)
                    if way == 0:
                        dve.wait_ge(a_edge_landed, 16)

                        n = v.n
                        with dve.Fori(0, EDGE_STEPS) as step:
                            for half in range(2):
                                dve.wait_ge(feat_landed[half], step * 16 + 16)
                                dve.tensor_tensor(feat[:, half, :, :], feat[:, half, :, :],
                                                  a_edge[:, :].unsqueeze(1).to_broadcast([EDGE_ROWS, CHUNK, ED]),
                                                  ALU.mult).then_inc(vdone, 1)
                                dve.wait_ge(vdone, step * 2 + (n + half + 1))
                                dve.tensor_reduce(recs[1][:, bass.ds(step * 2 * CHUNK + half * CHUNK, CHUNK), 3],
                                                  feat[:, half, :, :], AX.X, ALU.add).then_inc(feat_used, 1)
                        v.n += 2 * EDGE_STEPS
                        dve.wait_ge(feat_used, 2 * EDGE_STEPS)
                        dve.sem_inc(features_dotted, 1)

            @block.tensor
            def _(pe):
                def sum_counts(way):
                    pe.wait_ge(counted[way], 1)
                    nc.tensor.matmul(ps_count[:, way, 0, :], ones[:, :], count[:, :], start=True, stop=True)
                    nc.tensor.matmul(ps_count[:, way, 1, :], below[:, :], count[:, :], start=True, stop=True)\
                        .then_inc(count_summed[way], 1)

                def project(way, pair, buf):
                    t = pair * 2 + (way * NT + buf)
                    seen = (NT + 1 - buf) // 2 * way + 1
                    pe.wait_ge(xT_landed[buf], pair * 16 + seen * 16)
                    for g in range(2 * BLOCKS):
                        pe.wait_ge(proj_copied, t * (2 * BLOCKS) + (g + 1))
                        for k in range(KC):
                            r0 = g * 512 // D
                            last = nc.tensor.matmul(ps_proj[:, g % BANKS, :], xT[:, buf, k, :],
                                                    w_rel[:, k, r0:r0 + 512 // D, :], start=(k == 0), stop=(k == KC - 1))
                        last.then_inc(proj_summed, 1)

                for way in range(2):
                    sum_counts(way)
                    pe.wait_ge(w_landed, 16 * KC * (way + 1))
                    with pe.Fori(0, PAIRS) as pair:
                        project(way, pair, 0)
                        project(way, pair, 1)
                    for t in range(2 * PAIRS, NT):
                        project(way, t // 2, t % 2)
                pe.wait_ge(astray_found, 1)
                nc.tensor.matmul(ps_astray[:, :], ones[:, :], astray[:, :], start=True, stop=True).then_inc(astray_summed, 1)

            @block.scalar
            def _(act):
                act.sem_inc(proj_copied, BANKS)
                for way, w, table in ((0, Wb, table_b), (1, Wf, table_f)):
                    if way:
                        act.wait_ge(proj_summed, NT * 2 * BLOCKS)
                    for k in range(KC):
                        act.dma_start(w_rel[:, k, :, :], w[:, k * P:(k + 1) * P, :].rearrange("r i o -> i r o"))\
                            .then_inc(w_landed, 16)

                    def load_x(pair, buf):
                        act.dma_start(xT[:, buf, :, :], xT_pad[:, bass.ds(pair * 2 * P + buf * P, P)].rearrange("(k p) n -> p k n", p=P))\
                            .then_inc(xT_landed[buf], 16)

                    def tile(pair, buf, first, last):
                        t = pair * 2 + (way * NT + buf)
                        if not last:
                            load_x(pair + buf, 1 - buf)
                        for half in range(2):
                            if not first:
                                act.wait_ge(proj_stored[half], t * 16)
                            for g in range(half * BLOCKS, (half + 1) * BLOCKS):
                                act.wait_ge(proj_summed, t * (2 * BLOCKS) + (g + 1))
                                act.activation(proj[:, half, (g % BLOCKS) * 512:(g % BLOCKS + 1) * 512],
                                               ps_proj[:, g % BANKS, :], ACT.Copy).then_inc(proj_copied, 1)
                            act.wait_ge(proj_copied, t * (2 * BLOCKS) + ((half + 1) * BLOCKS + BANKS))
                            act.dma_start(table.ap()[bass.ds(pair * 2 * P + buf * P, P), half * HALF_W:(half + 1) * HALF_W],
                                          proj[:, half, :]).then_inc(proj_stored[half], 16)

                    load_x(0, 0)
                    tile(0, 0, way == 0, False)
                    tile(0, 1, False, False)
                    with act.Fori(1, PAIRS) as pair:
                        tile(pair, 0, False, False)
                        tile(pair, 1, False, False)
                    for t in range(2 * PAIRS, NT):
                        tile(t // 2, t % 2, False, t == NT - 1)
                for half in range(2):
                    act.wait_ge(proj_stored[half], 2 * NT * 16)
                act.wait_ge(owner_made, 2)
                act.dma_start(owner_b.ap().rearrange("(p c) -> p c", c=GC), owner_i[0][:, :]).then_inc(owner_stored, 16)
                act.dma_start(owner_f.ap().rearrange("(p c) -> p c", c=GC), owner_i[1][:, :]).then_inc(owner_stored, 16)
                act.dma_start(start_f.ap().rearrange("(p c) -> p c", c=GC), start_i[:, :]).then_inc(owner_stored, 16)
                act.dma_start(first_f.ap().rearrange("(p c) -> p c", c=GC), first[:, :]).then_inc(owner_stored, 16)

        slots_sb_b = sb("slots_sb_b", [P, T, 2])
        slots_sb_f = sb("slots_sb_f", [P, T, 4])
        owner_sb = [sb("owner_sb_b", [1, P * GC], I32), sb("owner_sb_f", [1, P * GC], I32)]
        acc_b = sb("acc_b", [P, NT * ROW])
        acc_f = sb("acc_f", [P, NT * ROW])
        rows_b = acc_b[:, :].rearrange("p (t w) -> p t w", w=ROW)
        rows_f = acc_f[:, :].rearrange("p (t w) -> p t w", w=ROW)

        with ExitStack() as two:
            gathered = sb("gathered", [P, RING, GROUP, ROW], scope=two)
            index = sb("index", [P, RING, GROUP], U32, two)
            local = sb("local", [P, RING, GROUP], scope=two)
            dot_e = sb("dot_e", [P, RING, GROUP], scope=two)
            start_sb = sb("start_sb", [1, P * GC], I32, two)
            slots_landed = sem("slots_landed")
            groups_landed = sem("groups_landed")
            first_landed = sem("first_landed")
            local_made = sem("local_made")

            def ring_of_sems(name):
                return [sem(f"{name}{q}") for q in range(RING)]

            cleared = sem("cleared")
            staged = ring_of_sems("staged")
            landed = ring_of_sems("landed")
            matched = ring_of_sems("matched")
            summed = ring_of_sems("summed")
            added = ring_of_sems("added")

            def add_messages(way, slots_sb, table, acc):
                turn0 = way * TURNS
                with ExitStack() as scope:
                    name = "bf"[way]
                    match = sb("match_" + name, [P, RING, GROUP, P], scope=scope)
                    if way == 1:
                        first_sb = sb("first_sb", [P, GROUPS], scope=scope)
                    ps_sum = psum("ps_sum_" + name, [P, RING, 512], scope)
                    block = scope.enter_context(nc.Block())

                    @block.sync
                    def _(sp):
                        if way == 0:
                            sp.dma_start(slots_sb_b[:, :, :], slots_b.ap().rearrange("(p t) w -> p t w", t=T)).then_inc(slots_landed, 16)
                            for per_group, there in ((owner_b, owner_sb[0]), (owner_f, owner_sb[1]), (start_f, start_sb)):
                                sp.dma_start(there[:, :], per_group.ap().rearrange("(a t) -> a t", a=1)).then_inc(slots_landed, 16)
                            sp.wait_ge(slots_landed, 64)
                            with sp.Fori(0, TURNS) as turn:
                                for q in range(RING):
                                    e0 = sp.value_load(start_sb[0:1, bass.ds(turn * RING + q, 1)], min_val=0, max_val=E)
                                    sp.dma_start(slots_sb_f[:, bass.ds(turn * (RING * GROUP) + q * GROUP, GROUP), :],
                                                 sorted_f.ap()[bass.ds(e0, SIZE), :].rearrange("(p u) w -> p u w", u=GROUP))\
                                        .then_inc(groups_landed, 16)
                            sp.wait_ge(groups_landed, 16 * GROUPS)
                        else:
                            sp.dma_start(first_sb[:, :], first_f.ap()[0:GROUPS].rearrange("(a t) -> a t", a=1).to_broadcast([P, GROUPS]))\
                                .then_inc(first_landed, 16)

                    @block.scalar
                    def _(act):
                        if way == 0:
                            for q in range(RING):
                                act.sem_inc(summed[q], 1)
                        act.wait_ge(slots_landed, 64)
                        if way == 1:
                            act.wait_ge(local_made, 1)
                        with act.Fori(turn0, turn0 + TURNS) as turn:
                            for q in range(RING):
                                act.wait_ge(summed[q], turn + 1)
                                there = bass.ds((turn - turn0) * (RING * GROUP) + q * GROUP, GROUP)
                                act.activation(index[:, q, :], slots_sb[:, there, 0], ACT.Copy)
                                act.activation(local[:, q, :], slots_sb[:, there, 1], ACT.Copy).then_inc(staged[q], 1)

                    @block.gpsimd
                    def _(pool):
                        pool.wait_ge(cleared, way * 2 + 2)
                        with pool.Fori(turn0, turn0 + TURNS) as turn:
                            for q in range(RING):
                                pool.wait_ge(staged[q], turn + 1)
                                pool.nop(nofuse=True)
                                for u in range(GROUP):
                                    pool.indirect_dma_start(
                                        gathered[:, q, u, 0:D], None, table,
                                        bass.IndirectOffsetOnAxis(ap=index[:, q, u:u + 1], axis=0)).then_inc(landed[q], 16)
                        for q in range(RING):
                            pool.wait_ge(landed[q], (turn0 + TURNS) * GROUP * 16)

                    @block.vector
                    def _(dve):
                        dve.memset(acc[:, :], 0.0).then_inc(cleared, 1)
                        dve.memset(gathered[:, :, :, COUNT], 1.0).then_inc(cleared, 1)
                        dve.wait_ge(cleared, way * 2 + 2)
                        dve.wait_ge(slots_landed, 64)
                        if way == 1:
                            dve.wait_ge(first_landed, 16)
                            nodes = slots_sb_f[:, :, 1].rearrange("p (g u) -> p g u", u=GROUP)
                            dve.tensor_tensor(nodes, nodes, first_sb[:, :].unsqueeze(2).to_broadcast([P, GROUPS, GROUP]),
                                              ALU.subtract).then_inc(local_made, 1)
                        else:
                            for q in range(RING):
                                dve.sem_inc(added[q], 1)

                        def match_group(turn, q):
                            dve.wait_ge(staged[q], turn + 1)
                            for u in range(GROUP):
                                last = dve.tensor_scalar(match[:, q, u, :], iota[:, :], local[:, q, u:u + 1], None, ALU.is_equal)
                            last.then_inc(matched[q], 1)

                        def add(turn, q):
                            at = dve.value_load(owner_sb[way][0:1, bass.ds((turn - turn0) * RING + q, 1)],
                                                min_val=0, max_val=(NT - 1) * ROW)
                            if q:
                                dve.wait_ge(added[q - 1], turn + 2)
                            else:
                                dve.wait_ge(added[RING - 1], turn + 1)
                            dve.wait_ge(summed[q], turn + 2)
                            dve.tensor_tensor(acc[:, bass.ds(at, COUNT + 1)], acc[:, bass.ds(at, COUNT + 1)],
                                              ps_sum[:, q, 0:COUNT + 1], ALU.add).then_inc(added[q], 1)

                        with dve.Fori(turn0, turn0 + TURNS) as turn:
                            match_group(turn, 0)
                            for q in range(1, RING):
                                match_group(turn, q)
                                add(turn, q - 1)
                            add(turn, RING - 1)

                    @block.tensor
                    def _(pe):
                        with pe.Fori(turn0, turn0 + TURNS) as turn:
                            for q in range(RING):
                                pe.wait_ge(landed[q], turn * (16 * GROUP) + 16 * GROUP)
                                pe.wait_ge(matched[q], turn + 1)
                                pe.wait_ge(added[q], turn + 1)
                                for u in range(GROUP):
                                    last = nc.tensor.matmul(ps_sum[:, q, 0:COUNT + 1], match[:, q, u, :],
                                                            gathered[:, q, u, 0:COUNT + 1],
                                                            start=(u == 0), stop=(u == GROUP - 1))
                                last.then_inc(summed[q], 1)

            add_messages(0, slots_sb_b, table_b.ap().rearrange("n (r d) -> (n r) d", d=D), acc_b)
            add_messages(1, slots_sb_f, table_f.ap().rearrange("n (r d) -> (n r) d", d=D), acc_f)

            with ExitStack() as three:
                def s3(name, shape, dt=F32):
                    return sb(name, shape, dt, three)

                x_rows = s3("x_rows", [P, D])
                x_cols = s3("x_cols", [P, KC, P])
                w_loop = s3("w_loop", [P, KC, D])
                bias = [s3("bias_b", [P, D]), s3("bias_f", [P, D]), s3("bias_s", [P, D])]
                w_att = s3("w_att", [P, KC, D])
                a_att = s3("a_att", [P, KC, 2])
                w_z = s3("w_z", [P, KC, D + 2])
                inv = [s3("inv_b", [P, NT]), s3("inv_f", [P, NT])]
                some = [s3("some_b", [P, NT]), s3("some_f", [P, NT])]
                h = s3("h", [P, D])
                fresh = s3("fresh", [P, ROW])
                stats = s3("stats", [P, 6])
                moments = s3("moments", [P, 2])
                eps = s3("eps", [P, 1])
                spread = s3("spread", [P, 1])
                x1 = s3("x1", [P, D])
                x1T = s3("x1T", [P, KC, P])
                z_row = s3("z_row", [P, DENOM + 1])
                ps_loop = psum("ps_loop", [P, 512], three)[:, 0:D]
                ps_u = psum("ps_u", [P, 512], three)[:, 0:2 * KC].rearrange("p (k j) -> p k j", j=2)
                ps_t = psum("ps_t", [P, 512], three)[:, 0:D].rearrange("p (k n) -> p k n", n=P)
                ps_z = psum("ps_z", [P, 512], three)[:, 0:D + 2]
                weights_landed = sem("weights_landed")
                x_landed = sem("x_landed")
                vnorm = sem("vnorm")
                u_summed = sem("u_summed")
                looped = sem("looped")
                std_made = sem("std_made")
                x1_made = sem("x1_made")
                x1_turned = sem("x1_turned")
                x1T_made = sem("x1T_made")
                z_summed = sem("z_summed")
                z_made = sem("z_made")
                z_stored = sem("z_stored")
                block = three.enter_context(nc.Block())
                STEPS = 12
                PRE = 12

                @block.sync
                def _(sp):
                    for k in range(KC):
                        rows = slice(k * P, (k + 1) * P)
                        sp.dma_start(w_loop[:, k, :], loop_weight[rows, :]).then_inc(weights_landed, 16)
                        sp.dma_start(w_att[:, k, :], W1[rows, :]).then_inc(weights_landed, 16)
                        sp.dma_start(w_z[:, k, 0:D], W1T[rows, :]).then_inc(weights_landed, 16)
                        for j in range(2):
                            sp.dma_start(a_att[:, k, j:j + 1], A1[0:1, j * D + k * P:j * D + (k + 1) * P].rearrange("a p -> p a"))\
                                .then_inc(weights_landed, 16)
                    for b, vec in zip(bias, (backward_bias, forward_bias, self_bias)):
                        sp.dma_start(b[:, :], vec.rearrange("(a n) -> a n", a=1).to_broadcast([P, D])).then_inc(weights_landed, 16)

                    def load(t):
                        sp.dma_start(x_rows[:, :], x_pad[bass.ds(t * P, P), :]).then_inc(x_landed, 16)
                        sp.dma_start(x_cols[:, :, :], xT_pad[:, bass.ds(t * P, P)].rearrange("(k p) n -> p k n", p=P))\
                            .then_inc(x_landed, 16)

                    load(0)
                    with sp.Fori(0, NT - 1) as t:
                        sp.wait_ge(x1_made, t + 1)
                        load(t + 1)
                        sp.wait_ge(z_made, t * 2 + 2)
                        sp.dma_start(z_table.ap()[bass.ds(t * P, P), :], z_row[:, :]).then_inc(z_stored, 16)
                    sp.wait_ge(z_made, NT * 2)
                    sp.dma_start(z_table.ap()[(NT - 1) * P:NT * P, :], z_row[:, :]).then_inc(z_stored, 16)
                    sp.wait_ge(z_stored, NT * 16)

                @block.tensor
                def _(pe):
                    pe.wait_ge(weights_landed, 16 * (5 * KC + 3))
                    for k in range(KC):
                        for j in range(KC):
                            last = nc.tensor.matmul(ps_u[:, k, :], w_att[:, j, k * P:(k + 1) * P], a_att[:, j, :],
                                                    start=(j == 0), stop=(j == KC - 1))
                    last.then_inc(u_summed, 1)
                    with pe.Fori(0, NT) as t:
                        pe.wait_ge(x_landed, t * 32 + 32)
                        for k in range(KC):
                            last = nc.tensor.matmul(ps_loop[:, :], x_cols[:, k, :], w_loop[:, k, :],
                                                    start=(k == 0), stop=(k == KC - 1))
                        last.then_inc(looped, 1)
                        pe.wait_ge(x1_made, t + 1)
                        for k in range(KC):
                            last = nc.tensor.transpose(ps_t[:, k, :], x1[:, k * P:(k + 1) * P], ident[:, :])
                        last.then_inc(x1_turned, 1)
                        pe.wait_ge(x1T_made, t + 1)
                        for k in range(KC):
                            last = nc.tensor.matmul(ps_z[:, :], x1T[:, k, :], w_z[:, k, :],
                                                    start=(k == 0), stop=(k == KC - 1))
                        last.then_inc(z_summed, 1)

                @block.scalar
                def _(act):
                    def tile(t, first):
                        act.wait_ge(vnorm, t * STEPS + (PRE + 9))
                        act.activation(spread[:, :], moments[:, 1:2], ACT.Sqrt, bias=eps[:, 0:1]).then_inc(std_made, 1)
                        act.wait_ge(x1_turned, t + 1)
                        act.activation(x1T[:, :, :], ps_t[:, :, :], ACT.Copy).then_inc(x1T_made, 1)
                        if not first:
                            act.wait_ge(z_stored, t * 16)
                        act.wait_ge(z_summed, t + 1)
                        act.activation(z_row[:, 0:COUNT + 1], ps_z[:, 0:COUNT + 1], ACT.Copy).then_inc(z_made, 1)

                    tile(0, True)
                    with act.Fori(1, NT) as t:
                        tile(t, False)

                @block.vector
                def _(dve):
                    v = Tally(vnorm)
                    v.up(dve.memset(eps[:, :], EPS))
                    v.up(dve.memset(z_row[:, DENOM:DENOM + 1], 1.0))
                    for way, rows in ((0, rows_b), (1, rows_f)):
                        v.up(dve.tensor_scalar(inv[way][:, :], rows[:, :, COUNT], 1.0, None, ALU.max))
                        dve.wait_ge(vnorm, v.n)
                        v.up(dve.reciprocal(inv[way][:, :], inv[way][:, :]))
                        v.up(dve.tensor_scalar(some[way][:, :], rows[:, :, COUNT], 1.0, None, ALU.min))
                    dve.wait_ge(weights_landed, 16 * (5 * KC + 3))
                    dve.wait_ge(u_summed, 1)
                    for k in range(KC):
                        v.up(dve.tensor_copy(w_z[:, k, D:D + 2], ps_u[:, k, :]))
                    v.up(dve.memset(fresh[:, 0:NEG_MAX], 0.0))
                    v.up(dve.memset(fresh[:, NEG_MAX:ROW], FLOOR))
                    n = v.n
                    assert n == PRE
                    with dve.Fori(0, NT) as t:
                        at = t * ROW
                        sums_b, sums_f = acc_b[:, bass.ds(at, D)], acc_f[:, bass.ds(at, D)]

                        def step(k):
                            dve.wait_ge(vnorm, t * STEPS + (n + k))

                        dve.wait_ge(x_landed, t * 32 + 32)
                        step(0)
                        dve.scalar_tensor_tensor(h[:, :], sums_f, inv[1][:, bass.ds(t, 1)], x_rows[:, :], ALU.mult, ALU.add).then_inc(vnorm, 1)
                        step(1)
                        dve.scalar_tensor_tensor(h[:, :], sums_b, inv[0][:, bass.ds(t, 1)], h[:, :], ALU.mult, ALU.add).then_inc(vnorm, 1)
                        dve.wait_ge(looped, t + 1)
                        step(2)
                        dve.scalar_tensor_tensor(h[:, :], ps_loop[:, :], 2.0, h[:, :], ALU.mult, ALU.add).then_inc(vnorm, 1)
                        for k, way in ((3, 0), (4, 1)):
                            step(k)
                            dve.scalar_tensor_tensor(h[:, :], bias[way][:, :], some[way][:, bass.ds(t, 1)], h[:, :],
                                                     ALU.mult, ALU.add).then_inc(vnorm, 1)
                        step(5)
                        dve.tensor_tensor(h[:, :], h[:, :], bias[2][:, :], ALU.add).then_inc(vnorm, 1)
                        step(6)
                        dve.bn_stats(stats[:, :], h[:, :]).then_inc(vnorm, 1)
                        step(7)
                        dve.nop(nofuse=True)
                        dve.bn_aggr(moments[:, :], stats[:, :]).then_inc(vnorm, 1)
                        step(8)
                        dve.tensor_scalar(acc_b[:, bass.ds(at, NEG_MAX)], fresh[:, 0:NEG_MAX], 1.0, None, ALU.mult).then_inc(vnorm, 1)
                        dve.wait_ge(std_made, t + 1)
                        step(9)
                        dve.reciprocal(spread[:, :], spread[:, :]).then_inc(vnorm, 1)
                        step(10)
                        dve.tensor_scalar(x1[:, :], h[:, :], moments[:, 0:1], spread[:, 0:1], ALU.subtract, ALU.mult)\
                            .then_inc(vnorm, 1)
                        step(11)
                        dve.tensor_scalar(acc_f[:, bass.ds(at, D)], x1[:, :], 1.0, None, ALU.mult).then_inc(x1_made, 1)
                        dve.tensor_scalar(acc_b[:, bass.ds(at + NEG_MAX, 1)], fresh[:, NEG_MAX:ROW - 1], 1.0, None, ALU.mult)\
                            .then_inc(vnorm, 1)
                        dve.wait_ge(z_made, t * 2 + 1)
                        dve.tensor_scalar(acc_b[:, bass.ds(at + S_DST, 1)], ps_z[:, D + 1:D + 2], 1.0, None, ALU.mult)\
                            .then_inc(z_made, 1)

            with ExitStack() as four:
                def s4(name, shape, dt=F32):
                    return sb(name, shape, dt, four)

                spread_e = s4("spread_e", [P, RING, GROUP, P])
                fifth = s4("fifth", [P, 2, SIZE])
                logit = s4("logit", [P, 2, SIZE])
                prob = s4("prob", [P, 2, GROUP, P])
                probT = s4("probT", [P, 2, SIZE])
                v_edge = s4("v_edge", [P, RING, GROUP])
                s_dst = s4("s_dst", [P, RING])
                s_fifth = s4("s_fifth", [P, RING])
                top = s4("top", [P, RING])
                neg_max = s4("neg_max", [P, RING])
                drop = s4("drop", [P, RING])
                shrink = s4("shrink", [P, RING])
                ps_v = psum("ps_v", [P, 2, 512], four)
                ps_p = psum("ps_p", [P, 2, 512], four)
                ps_o = psum("ps_o", [P, RING // 2, 512], four)
                v_made = ring_of_sems("v_made")
                spread_made = ring_of_sems("spread_made")
                v_turned = ring_of_sems("v_turned")
                fifth_made = ring_of_sems("fifth_made")
                logit_made = ring_of_sems("logit_made")
                top_made = ring_of_sems("top_made")
                lowered = ring_of_sems("lowered")
                dropped = ring_of_sems("dropped")
                maxed = ring_of_sems("maxed")
                prob_made = ring_of_sems("prob_made")
                prob_turned = ring_of_sems("prob_turned")
                probT_made = ring_of_sems("probT_made")
                turn0 = 2 * TURNS
                block = four.enter_context(nc.Block())

                def staggered(eng, stages, begin=lambda: None):
                    for q in range(RING):
                        for stage, lag in stages:
                            if q >= lag:
                                stage(0, q - lag)
                    with eng.Fori(1, TURNS) as turn:
                        begin()
                        for q in range(RING):
                            for stage, lag in stages:
                                if q >= lag:
                                    stage(turn, q - lag)
                                else:
                                    stage(turn - 1, q - lag + RING)
                    begin()
                    for q in range(max(lag for _, lag in stages)):
                        for stage, lag in stages:
                            if q < lag:
                                stage(TURNS - 1, q - lag + RING)

                @block.gpsimd
                def _(pool):
                    with pool.Fori(0, TURNS) as turn:
                        for q in range(RING):
                            pool.wait_ge(staged[q], turn + (turn0 + 1))
                            pool.nop(nofuse=True)
                            for u in range(GROUP):
                                pool.indirect_dma_start(
                                    gathered[:, q, u, 0:DENOM + 1], None, z_table.ap(),
                                    bass.IndirectOffsetOnAxis(ap=index[:, q, u:u + 1], axis=0)).then_inc(landed[q], 16)
                    for q in range(RING):
                        pool.wait_ge(landed[q], (turn0 + TURNS) * GROUP * 16)

                @block.scalar
                def _(act):
                    for q in range(RING):
                        act.sem_inc(probT_made[q], 1)

                    def stage(turn, q):
                        act.wait_ge(summed[q], turn + (turn0 + 1))
                        there = bass.ds(turn * (RING * GROUP) + q * GROUP, GROUP)
                        act.activation(index[:, q, :], slots_sb_f[:, there, 2], ACT.Copy)
                        act.activation(local[:, q, :], slots_sb_f[:, there, 1], ACT.Copy)
                        act.activation(dot_e[:, q, :], slots_sb_f[:, there, 3], ACT.Copy).then_inc(staged[q], 1)
                        at = act.value_load(owner_sb[1][0:1, bass.ds(turn * RING + q, 1)], min_val=0, max_val=(NT - 1) * ROW)
                        act.activation(s_dst[:, q:q + 1], acc_b[:, bass.ds(at + S_DST, 1)], ACT.Copy)
                        act.activation(s_fifth[:, q:q + 1], acc_b[:, bass.ds(at + S_DST, 1)], ACT.Copy, scale=ALPHA)

                    def add_v(turn, q):
                        act.wait_ge(v_made[q], turn + 1)
                        for u in range(GROUP):
                            last = act.activation(spread_e[:, q, u, :], spread_e[:, q, u, :], ACT.Identity,
                                                  bias=v_edge[:, q, u:u + 1])
                        last.then_inc(spread_made[q], 1)

                    def make_fifth(turn, q):
                        act.wait_ge(v_turned[q], turn + 1)
                        act.activation(fifth[:, q % 2, :], ps_v[:, q % 2, :], ACT.Identity, scale=ALPHA,
                                       bias=s_fifth[:, q:q + 1]).then_inc(fifth_made[q], 1)

                    def to_prob(turn, q):
                        act.wait_ge(maxed[q], turn + 1)
                        act.activation(prob[:, q % 2, :, :].rearrange("p u e -> p (u e)"), logit[:, q % 2, :], ACT.Exp,
                                       bias=neg_max[:, q:q + 1])
                        act.activation(shrink[:, q:q + 1], drop[:, q:q + 1], ACT.Exp).then_inc(prob_made[q], 1)

                    def copy_probT(turn, q):
                        act.wait_ge(prob_turned[q], turn + 1)
                        act.activation(probT[:, q % 2, :], ps_p[:, q % 2, :], ACT.Copy).then_inc(probT_made[q], 1)

                    staggered(act, [(add_v, 4), (to_prob, 5), (make_fifth, 4), (stage, 0), (copy_probT, 5)])

                @block.vector
                def _(dve):
                    kept = {}

                    def owner_of(turn, q):
                        return dve.value_load(owner_sb[1][0:1, bass.ds(turn * RING + q, 1)], min_val=0, max_val=(NT - 1) * ROW)

                    def mask(turn, q):
                        dve.wait_ge(staged[q], turn + (turn0 + 1))
                        for u in range(GROUP):
                            dve.tensor_scalar(spread_e[:, q, u, :], iota[:, :], local[:, q, u:u + 1], -FAR,
                                              ALU.not_equal, ALU.mult)

                    def make_v(turn, q):
                        dve.wait_ge(landed[q], turn * (16 * GROUP) + (turn0 + 1) * 16 * GROUP)
                        dve.tensor_tensor(v_edge[:, q, :], gathered[:, q, :, D], dot_e[:, q, :], ALU.add).then_inc(v_made[q], 1)

                    def new_max(turn, q):
                        at = kept[q] = owner_of(turn, q)
                        old = acc_b[:, bass.ds(at + NEG_MAX, 1)]
                        dve.wait_ge(fifth_made[q], turn + 1)
                        dve.scalar_tensor_tensor(logit[:, q % 2, :], ps_v[:, q % 2, :], s_dst[:, q:q + 1], fifth[:, q % 2, :],
                                                 ALU.add, ALU.max).then_inc(logit_made[q], 1)
                        dve.wait_ge(logit_made[q], turn + 1)
                        dve.tensor_reduce(top[:, q:q + 1], logit[:, q % 2, :], AX.X, ALU.max).then_inc(top_made[q], 1)
                        dve.wait_ge(top_made[q], turn + 1)
                        if q:
                            dve.wait_ge(maxed[q - 1], turn + 1)
                        elif not isinstance(turn, int) or turn:
                            dve.wait_ge(maxed[RING - 1], turn)
                        dve.scalar_tensor_tensor(neg_max[:, q:q + 1], top[:, q:q + 1], -1.0, old, ALU.mult, ALU.min)\
                            .then_inc(lowered[q], 1)
                        dve.wait_ge(lowered[q], turn + 1)
                        dve.tensor_tensor(drop[:, q:q + 1], neg_max[:, q:q + 1], old, ALU.subtract).then_inc(dropped[q], 1)
                        dve.wait_ge(dropped[q], turn + 1)
                        dve.tensor_scalar(old, neg_max[:, q:q + 1], 1.0, None, ALU.mult).then_inc(maxed[q], 1)

                    def add(turn, q):
                        at = kept.pop(q) if q in kept else owner_of(turn, q)
                        sums = acc_b[:, bass.ds(at, DENOM + 1)]
                        if q:
                            dve.wait_ge(added[q - 1], turn + (turn0 + 2))
                        else:
                            dve.wait_ge(added[RING - 1], turn + (turn0 + 1))
                        dve.wait_ge(summed[q], turn + (turn0 + 2))
                        dve.scalar_tensor_tensor(sums, sums, shrink[:, q:q + 1], ps_o[:, q % (RING // 2), 0:DENOM + 1],
                                                 ALU.mult, ALU.add).then_inc(added[q], 1)

                    staggered(dve, [(mask, 3), (make_v, 3), (new_max, 5), (add, 6)], kept.clear)

                @block.tensor
                def _(pe):
                    def turn_v(turn, q):
                        pe.wait_ge(spread_made[q], turn + 1)
                        if q >= 2:
                            pe.wait_ge(logit_made[q - 2], turn + 1)
                        elif not isinstance(turn, int) or turn:
                            pe.wait_ge(logit_made[q - 2 + RING], turn)
                        for u in range(GROUP):
                            last = nc.tensor.transpose(ps_v[:, q % 2, u * P:(u + 1) * P], spread_e[:, q, u, :], ident[:, :])
                        last.then_inc(v_turned[q], 1)

                    def turn_prob(turn, q):
                        pe.wait_ge(prob_made[q], turn + 1)
                        if q >= 2:
                            pe.wait_ge(probT_made[q - 2], turn + 2)
                        else:
                            pe.wait_ge(probT_made[q - 2 + RING], turn + 1)
                        for u in range(GROUP):
                            last = nc.tensor.transpose(ps_p[:, q % 2, u * P:(u + 1) * P], prob[:, q % 2, u, :], ident[:, :])
                        last.then_inc(prob_turned[q], 1)

                    def sum_up(turn, q):
                        if q >= RING // 2:
                            pe.wait_ge(added[q - RING // 2], turn + (turn0 + 2))
                        else:
                            pe.wait_ge(added[q + RING // 2], turn + (turn0 + 1))
                        pe.wait_ge(probT_made[q], turn + 2)
                        for u in range(GROUP):
                            last = nc.tensor.matmul(ps_o[:, q % (RING // 2), 0:DENOM + 1], probT[:, q % 2, u * P:(u + 1) * P],
                                                    gathered[:, q, u, 0:DENOM + 1], start=(u == 0), stop=(u == GROUP - 1))
                        last.then_inc(summed[q], 1)

                    staggered(pe, [(turn_v, 4), (turn_prob, 5), (sum_up, 5)])

        with ExitStack() as five:
            h = sb("h2", [P, D], scope=five)
            stats = sb("stats2", [P, 6], scope=five)
            moments = sb("moments2", [P, 2], scope=five)
            eps = sb("eps2", [P, 1], scope=five)
            spread = sb("spread2", [P, 1], scope=five)
            inv = sb("inv2", [P, NT], scope=five)
            vlast = sem("vlast")
            std_made = sem("std2_made")
            out_stored = sem("out_stored")
            block = five.enter_context(nc.Block())

            @block.sync
            def _(sp):
                with sp.Fori(0, NT) as t:
                    sp.wait_ge(vlast, t * 5 + 8)
                    sp.dma_start(out[bass.ds(t * P, P), :], acc_f[:, bass.ds(t * ROW, D)]).then_inc(out_stored, 16)
                sp.wait_ge(out_stored, NT * 16)

            @block.scalar
            def _(act):
                with act.Fori(0, NT) as t:
                    act.wait_ge(vlast, t * 5 + 6)
                    act.activation(spread[:, :], moments[:, 1:2], ACT.Sqrt, bias=eps[:, 0:1]).then_inc(std_made, 1)

            @block.vector
            def _(dve):
                dve.memset(eps[:, :], EPS).then_inc(vlast, 1)
                dve.tensor_scalar(inv[:, :], rows_b[:, :, DENOM], 1e-30, None, ALU.max).then_inc(vlast, 1)
                dve.wait_ge(vlast, 2)
                dve.reciprocal(inv[:, :], inv[:, :]).then_inc(vlast, 1)
                with dve.Fori(0, NT) as t:
                    x1 = acc_f[:, bass.ds(t * ROW, D)]
                    dve.wait_ge(vlast, t * 5 + 3)
                    dve.scalar_tensor_tensor(h[:, :], acc_b[:, bass.ds(t * ROW, D)], inv[:, bass.ds(t, 1)], x1,
                                             ALU.mult, ALU.add).then_inc(vlast, 1)
                    dve.wait_ge(vlast, t * 5 + 4)
                    dve.bn_stats(stats[:, :], h[:, :]).then_inc(vlast, 1)
                    dve.wait_ge(vlast, t * 5 + 5)
                    dve.nop(nofuse=True)
                    dve.bn_aggr(moments[:, :], stats[:, :]).then_inc(vlast, 1)
                    dve.wait_ge(std_made, t + 1)
                    dve.reciprocal(spread[:, :], spread[:, :]).then_inc(vlast, 1)
                    dve.wait_ge(vlast, t * 5 + 7)
                    dve.tensor_scalar(x1, h[:, :], moments[:, 0:1], spread[:, 0:1], ALU.subtract, ALU.mult)\
                        .then_inc(vlast, 1)


_INS = ["x_pad", "xT_pad", "src", "dst", "edge_attr_64", "edge_type_16", "L0_gnn_Wf", "L0_gnn_Wb",
        "L0_gnn_loop_weight", "L0_gnn_forward_bias", "L0_gnn_backward_bias", "L0_gnn_self_bias",
        "L1_gnn_W", "L1_gnn_WT", "L1_gnn_A"]


def kernel(**inputs):
    import numpy as _np
    import concourse.bacc as _bacc
    from concourse import mybir as _mybir
    from concourse.bass_utils import run_bass_kernel_spmd as _run

    n, d = inputs["x"].shape
    n_pad = -(-n // 128) * 128
    x_pad = _np.zeros((n_pad, d), _np.float32)
    x_pad[:n] = inputs["x"]
    laid = dict(inputs)
    laid["x_pad"] = x_pad
    laid["xT_pad"] = x_pad.T
    laid["L1_gnn_WT"] = _np.asarray(inputs["L1_gnn_W"]).T

    nc = _bacc.Bacc("TRN2", target_bir_lowering=False, num_devices=1)
    arrays, args = {}, []
    for name in _INS:
        a = _np.ascontiguousarray(laid[name])
        arrays[f"in_{name}_dram"] = a
        args.append(nc.dram_tensor(f"in_{name}_dram", a.shape, _mybir.dt.from_np(a.dtype), kind="ExternalInput").ap())
    out = nc.dram_tensor("out_0_dram", (n_pad, d), _mybir.dt.float32, kind="ExternalOutput").ap()
    gnn(nc, *args, out)
    r = _run(nc, [arrays], core_ids=[0])
    return r.results[0]["out_0_dram"][:n]
```

```python
from contextlib import ExitStack

import concourse.bass as bass
from concourse import mybir

P = 128
F32 = mybir.dt.float32
BF16 = mybir.dt.bfloat16
I32 = mybir.dt.int32
U32 = mybir.dt.uint32
U16 = mybir.dt.uint16
ALU = mybir.AluOpType
ACT = mybir.ActivationFunctionType
AX = mybir.AxisListType

EDGE_ROWS = 125
HALF = 15
GROUP_M = 2
GROUP = 4
RING = 6
BANKS = 4
ROW = 260
COUNT = 256
DENOM = 257
NEG_MAX = 258
S_DST = 259
EPS = 1e-5
ALPHA = 0.2
FAR = 1e30
FLOOR = 1e28


class Tally:

    def __init__(self, sem):
        self.sem, self.n = sem, 0

    def up(self, instruction):
        instruction.then_inc(self.sem, 1)
        self.n += 1


def gnn(nc, x_pad, xT_pad, src, dst, edge_attr, edge_type, Wf, Wb, loop_weight, forward_bias,
        backward_bias, self_bias, W1, W1T, A1, out):
    NPAD, D = x_pad.shape
    E, ED = edge_attr.shape
    R = Wf.shape[0]
    KC = D // P
    NT = NPAD // P
    EC = E // EDGE_ROWS
    assert EC * EDGE_ROWS == E and EC % (2 * HALF) == 0 and D == 2 * P and R * D % 1024 == 0
    SIZE_M, SIZE = GROUP_M * P, GROUP * P

    def turns_of(size):
        return -(-((E + NT * (size - 1)) // size) // RING)

    TURNS_M, TURNS = turns_of(SIZE_M), turns_of(SIZE)
    GROUPS_M, GROUPS = TURNS_M * RING, TURNS * RING
    GC_M, GC = -(-GROUPS_M // P), -(-GROUPS // P)
    T_M, T = GROUPS_M * GROUP_M, GROUPS * GROUP
    BLANK = max(b for b in range(1, 65) if T_M % b == 0)
    TURNS_BEFORE = (0, TURNS_M, 2 * TURNS_M)
    LANDED_BEFORE = (0, 16 * GROUP_M * TURNS_M, 32 * GROUP_M * TURNS_M)
    SCATTER_STEPS = EC // (2 * HALF)
    EDGE_STEPS = max(2, SCATTER_STEPS // 5)
    HEAD = EDGE_STEPS * 2 * HALF
    assert 2 * EDGE_STEPS <= SCATTER_STEPS
    CHUNK = EC // (2 * EDGE_STEPS)
    PAIRS = (NT - 1) // 2
    assert CHUNK * 2 * EDGE_STEPS == EC and PAIRS > 1
    HALF_W = R * D // 2
    BLOCKS = HALF_W // 512

    table_f = nc.dram_tensor("table_f", (NPAD, R * D), F32)
    table_b = nc.dram_tensor("table_b", (NPAD, R * D), F32)
    z_table = nc.dram_tensor("z_table", (NPAD, DENOM + 1), F32)
    slots_b = nc.dram_tensor("slots_b", (P * T_M, 2), F32)
    sorted_f = nc.dram_tensor("sorted_f", (E + SIZE, 4), F32)
    owner_b = nc.dram_tensor("owner_b", (P * GC_M,), I32)
    owner_m = nc.dram_tensor("owner_m", (P * GC_M,), I32)
    start_m = nc.dram_tensor("start_m", (P * GC_M,), I32)
    first_m = nc.dram_tensor("first_m", (P * GC_M,), F32)
    owner_a = nc.dram_tensor("owner_a", (P * GC,), I32)
    start_a = nc.dram_tensor("start_a", (P * GC,), I32)
    first_a = nc.dram_tensor("first_a", (P * GC,), F32)

    with ExitStack() as whole:
        def sem(name):
            return whole.enter_context(nc.semaphore(name))

        def sb(name, shape, dt=F32, scope=whole):
            return scope.enter_context(nc.sbuf_tensor(name, shape, dt))

        def psum(name, shape, scope):
            return scope.enter_context(nc.psum_tensor(name, shape, F32))

        iota = sb("iota", [P, P])
        iota_i = sb("iota_i", [P, P], I32)
        row_i = sb("row_i", [P, 1], I32)
        row_f = sb("row_f", [P, 1])
        ident = sb("ident", [P, P])

        def in_register(eng, value):
            return value if isinstance(value, int) else eng.snap(value)

        with ExitStack() as one:
            def s1(name, shape, dt=F32):
                return sb(name, shape, dt, one)

            src_i = s1("src_i", [EDGE_ROWS, EC], I32)
            dst_i = s1("dst_i", [EDGE_ROWS, EC], I32)
            type_i = s1("type_i", [EDGE_ROWS, EC], I32)
            feat = s1("feat", [EDGE_ROWS, 2, CHUNK, ED])
            a_edge = s1("a_edge", [EDGE_ROWS, ED])
            work_i = s1("work_i", [EDGE_ROWS, EC], I32)
            bucket = s1("bucket", [EDGE_ROWS, EC], BF16)
            inside = s1("inside", [EDGE_ROWS, EC], U16)
            ranks = s1("ranks", [EDGE_ROWS, EC])
            place = s1("place", [EDGE_ROWS, EC])
            nil = s1("nil", [EDGE_ROWS, 1])
            edge_i = s1("edge_i", [EDGE_ROWS, EC], I32)
            astray = s1("astray", [EDGE_ROWS, 1])
            astray_i = s1("astray_i", [1, 1], I32)
            addr = [s1("addr_b", [EDGE_ROWS, EC], U32), s1("addr_f", [EDGE_ROWS, EC], U32)]
            recs = [s1("recs_b", [EDGE_ROWS, EC, 2]), s1("recs_f", [EDGE_ROWS, EC, 4])]
            below = s1("below", [EDGE_ROWS, P])
            ones = s1("ones", [EDGE_ROWS, P])
            group_i = [s1("group_ib", [P, GC_M], I32), s1("group_if", [P, GC], I32)]
            group_f = [s1("group_fb", [P, GC_M]), s1("group_ff", [P, GC])]
            count = s1("count", [EDGE_ROWS, NT])
            groups_i = s1("groups_i", [P, NT], I32)
            groups = s1("groups", [P, NT])
            tend = s1("tend", [P, NT])
            base = s1("base", [P, NT])
            all_past = s1("past", [P, GC_M, NT])
            all_owner = s1("owner", [P, GC_M])
            owner_i = [s1("owner_ib", [P, GC_M], I32), s1("owner_im", [P, GC_M], I32), s1("owner_ia", [P, GC], I32)]
            nil_t = s1("nil_t", [P, NT])
            spare = s1("spare", [P, NT])
            all_start = s1("start", [P, GC_M])
            start_i = [s1("start_im", [P, GC_M], I32), s1("start_ia", [P, GC], I32)]
            first = [s1("first_m_sb", [P, GC_M]), s1("first_a_sb", [P, GC])]
            blank_b = s1("blank_b", [P, BLANK, 2])
            blank_f = s1("blank_f", [P, GROUP, 4])
            w_rel = s1("w_rel", [P, KC, R, D])
            xT = s1("xT", [P, 2, KC, P])
            proj = s1("proj", [P, 2, HALF_W])
            stage_rec = [s1("stage_recb", [EDGE_ROWS, 2, HALF, 2]), s1("stage_recf", [EDGE_ROWS, 2, HALF, 4])]
            stage_addr = s1("stage_addr", [EDGE_ROWS, 2, HALF], U32)
            ps_proj = psum("ps_proj", [P, BANKS, 512], one)
            ps_count = psum("ps_count", [P, 512], one)[:, 0:4 * NT].rearrange("p (w k t) -> p w k t", w=2, k=2)
            ps_astray = psum("ps_astray", [P, 512], one)[:, 0:1]

            inputs_landed = sem("inputs_landed")
            feat_landed = [sem("feat_landed0"), sem("feat_landed1")]
            feat_used = sem("feat_used")
            iotas = sem("iotas")
            blanks = sem("blanks")
            blank_stored = sem("blank_stored")
            vdone = sem("vdone")
            counted = [sem("counted_b"), sem("counted_f")]
            count_summed = [sem("count_summed_b"), sem("count_summed_f")]
            astray_found = sem("astray_found")
            astray_summed = sem("astray_summed")
            astray_known = sem("astray_known")
            edges_stored = sem("edges_stored")
            owner_made = sem("owner_made")
            owner_stored = sem("owner_stored")
            placed = [sem("placed_b"), sem("placed_f")]
            features_dotted = sem("features_dotted")
            staged = [sem("scatter_staged0"), sem("scatter_staged1")]
            scattered = [sem("scattered0"), sem("scattered1")]
            w_landed = sem("w_landed")
            xT_landed = [sem("xT_landed0"), sem("xT_landed1")]
            proj_summed = sem("proj_summed")
            proj_copied = sem("proj_copied")
            proj_stored = [sem("proj_stored0"), sem("proj_stored1")]

            block = one.enter_context(nc.Block())

            @block.sync
            def _(sp):
                sp.dma_start(src_i[:, :], src.rearrange("(p c) -> p c", c=EC)).then_inc(inputs_landed, 16)
                sp.dma_start(dst_i[:, :], dst.rearrange("(p c) -> p c", c=EC)).then_inc(inputs_landed, 16)
                sp.dma_start(type_i[:, :], edge_type.rearrange("(p c) -> p c", c=EC)).then_inc(inputs_landed, 16)
                sp.dma_start(a_edge[:, :], A1[:, 2 * D:].to_broadcast([EDGE_ROWS, ED])).then_inc(inputs_landed, 16)
                sp.wait_ge(blanks, 4)
                blank_rows_b = slots_b.ap().rearrange("(p t) w -> p t w", t=T_M)
                for c in range(T_M // BLANK):
                    here = slice(c * BLANK, (c + 1) * BLANK)
                    sp.dma_start(blank_rows_b[:, here, :], blank_b[:, :, :]).then_inc(blank_stored, 16)

                sp.dma_start(sorted_f.ap()[E:E + SIZE, :].rearrange("(p u) w -> p u w", u=GROUP), blank_f[:, :, :])\
                    .then_inc(blank_stored, 16)

                feat_rows = edge_attr.rearrange("(p c) f -> p c f", c=EC)

                def load_features(step, half):
                    sp.dma_start(feat[:, half, :, :], feat_rows[:, bass.ds(step * 2 * CHUNK + half * CHUNK, CHUNK), :])\
                        .then_inc(feat_landed[half], 16)

                def stage(way, step, half):
                    c0 = step * 2 * HALF + half * HALF
                    sp.dma_start(stage_rec[way][:, half, :, :], recs[way][:, bass.ds(c0, HALF), :]).then_inc(staged[half], 16)
                    sp.dma_start(stage_addr[:, half, :], addr[way][:, bass.ds(c0, HALF)]).then_inc(staged[half], 16)

                load_features(0, 0)
                load_features(0, 1)
                sp.wait_ge(placed[0], 1)
                stage(0, 0, 0)
                stage(0, 0, 1)
                with sp.Fori(1, EDGE_STEPS) as step:
                    for half in range(2):
                        sp.wait_ge(scattered[half], step * 16 * HALF)
                        stage(0, step, half)
                sp.wait_ge(placed[0], 2)
                with sp.Fori(EDGE_STEPS, 2 * EDGE_STEPS - 1) as step:
                    for half in range(2):
                        sp.wait_ge(scattered[half], step * 16 * HALF)
                        stage(0, step, half)
                    for half in range(2):
                        sp.wait_ge(feat_used, (step - EDGE_STEPS) * 2 + (half + 1))
                        load_features(step - (EDGE_STEPS - 1), half)
                with sp.Fori(2 * EDGE_STEPS - 1, SCATTER_STEPS) as step:
                    for half in range(2):
                        sp.wait_ge(scattered[half], step * 16 * HALF)
                        stage(0, step, half)
                sp.wait_ge(placed[1], 1)
                sp.wait_ge(features_dotted, 1)
                sp.wait_ge(astray_known, 1)
                moved = sp.alloc_register("moved_sp")
                sp.reg_load(moved, astray_i[0:1, 0:1])
                with sp.If_ne(moved, 0):
                    with sp.Fori(0, SCATTER_STEPS) as step:
                        for half in range(2):
                            sp.wait_ge(scattered[half], (step + SCATTER_STEPS) * 16 * HALF)
                            stage(1, step, half)
                with sp.Else():
                    sp.dma_start(sorted_f.ap()[0:E, :].rearrange("(p c) w -> p c w", c=EC), recs[1][:, :, :])\
                        .then_inc(edges_stored, 16)
                    sp.wait_ge(edges_stored, 16)
                sp.wait_ge(owner_stored, 7 * 16)

            @block.gpsimd
            def _(pool):
                pool.iota(iota_i[:, :], pattern=[[1, P]], base=0, channel_multiplier=0).then_inc(iotas, 1)
                pool.iota(row_i[:, :], pattern=[[0, 1]], base=0, channel_multiplier=1).then_inc(iotas, 1)
                for numbers, columns in zip(group_i, (GC_M, GC)):
                    pool.iota(numbers[:, :], pattern=[[1, columns]], base=0, channel_multiplier=columns).then_inc(iotas, 1)
                pool.iota(edge_i[:, :], pattern=[[1, EC]], base=1, channel_multiplier=EC).then_inc(iotas, 1)
                pool.memset(blank_b[:, :, 0], 0.0).then_inc(blanks, 1)
                pool.memset(blank_b[:, :, 1], -1.0).then_inc(blanks, 1)
                pool.memset(blank_f[:, :, 0:4], 0.0).then_inc(blanks, 1)
                pool.wait_ge(blanks, 3)
                pool.memset(blank_f[:, :, 2], -1.0).then_inc(blanks, 1)
                pool.wait_ge(blank_stored, 16 * (T_M // BLANK + 1))

                def scatter_all(way, slots):
                    def scatter(half):
                        for c in range(HALF):
                            pool.indirect_dma_start(
                                slots.ap(), bass.IndirectOffsetOnAxis(ap=stage_addr[:, half, c:c + 1], axis=0),
                                stage_rec[way][:, half, c, :], None).then_inc(scattered[half], 16)

                    with pool.Fori(0, SCATTER_STEPS) as step:
                        for half in range(2):
                            pool.wait_ge(staged[half], step * 32 + (way * SCATTER_STEPS + 1) * 32)
                            pool.nop(nofuse=True)
                            scatter(half)
                    for half in range(2):
                        pool.wait_ge(scattered[half], (way + 1) * SCATTER_STEPS * HALF * 16)

                scatter_all(0, slots_b)
                pool.wait_ge(astray_known, 1)
                moved = pool.alloc_register("moved_pool")
                pool.reg_load(moved, astray_i[0:1, 0:1])
                with pool.If_ne(moved, 0):
                    scatter_all(1, sorted_f)

            @block.vector
            def _(dve):
                v = Tally(vdone)
                dve.wait_ge(iotas, 5)
                v.up(dve.tensor_copy(iota[:, :], iota_i[:, :]))
                v.up(dve.tensor_copy(row_f[:, :], row_i[:, :]))
                for whole_numbers, numbers in zip(group_i, group_f):
                    v.up(dve.tensor_copy(numbers[:, :], whole_numbers[:, :]))
                v.up(dve.memset(ones[:, :], 1.0))
                v.up(dve.memset(nil[:, :], 0.0))
                v.up(dve.memset(nil_t[:, :], 0.0))
                dve.wait_ge(vdone, v.n)
                v.up(dve.tensor_scalar(ident[:, :], iota[:, :], row_f[:, 0:1], None, ALU.is_equal))
                v.up(dve.tensor_scalar(below[:, :], iota[0:EDGE_ROWS, :], row_f[0:EDGE_ROWS, 0:1], None, ALU.is_gt))
                dve.wait_ge(inputs_landed, 64)

                def end_buckets(way, size):
                    dve.wait_ge(vdone, v.n)
                    v.up(dve.tensor_scalar(groups[:, :], ps_count[:, way, 0, :], float(size - 1), None, ALU.add))
                    dve.wait_ge(vdone, v.n)
                    v.up(dve.tensor_copy(groups_i[:, :], groups[:, :]))
                    dve.wait_ge(vdone, v.n)
                    v.up(dve.tensor_scalar(groups_i[:, :], groups_i[:, :], size.bit_length() - 1, None, ALU.logical_shift_right))
                    dve.wait_ge(vdone, v.n)
                    v.up(dve.tensor_copy(groups[:, :], groups_i[:, :]))
                    dve.wait_ge(vdone, v.n)
                    v.up(dve.tensor_tensor_scan(tend[:, :], groups[:, :], nil_t[:, :], 0.0, ALU.add, ALU.add))
                    dve.wait_ge(vdone, v.n)

                def find_owners(numbers, columns, owners):
                    past, owner = all_past[:, 0:columns, :], all_owner[:, 0:columns]
                    v.up(dve.tensor_tensor(past, numbers[:, :].unsqueeze(2).to_broadcast([P, columns, NT]),
                                           tend[:, :].unsqueeze(1).to_broadcast([P, columns, NT]), ALU.is_ge))
                    dve.wait_ge(vdone, v.n)
                    v.up(dve.tensor_reduce(owner, past, AX.X, ALU.add))
                    dve.wait_ge(vdone, v.n)
                    v.up(dve.tensor_scalar(owners[:, :], owner, float(NT - 1), float(ROW), ALU.min, ALU.mult))

                def find_starts(way, size, numbers, columns, firsts, starts):
                    past, owner, start = all_past[:, 0:columns, :], all_owner[:, 0:columns], all_start[:, 0:columns]
                    v.up(dve.scalar_tensor_tensor(spare[:, :], groups[:, :], -float(size), ps_count[:, way, 0, :], ALU.mult, ALU.add))
                    v.up(dve.tensor_scalar(firsts[:, :], owner, float(NT - 1), float(P), ALU.min, ALU.mult))
                    dve.wait_ge(vdone, v.n)
                    v.up(dve.tensor_tensor(past, past, spare[:, :].unsqueeze(1).to_broadcast([P, columns, NT]), ALU.mult))
                    dve.wait_ge(vdone, v.n)
                    v.up(dve.tensor_reduce(start, past, AX.X, ALU.add))
                    dve.wait_ge(vdone, v.n)
                    v.up(dve.scalar_tensor_tensor(start, numbers[:, :], float(size), start, ALU.mult, ALU.add))
                    dve.wait_ge(vdone, v.n)
                    v.up(dve.tensor_scalar(starts[:, :], start, float(E), None, ALU.min))
                    dve.wait_ge(vdone, v.n)

                for way, key, other in ((0, src_i, dst_i), (1, dst_i, src_i)):
                    dve.wait_ge(vdone, v.n)
                    v.up(dve.tensor_scalar(work_i[:, :], key[:, :], 7, None, ALU.logical_shift_right))
                    dve.wait_ge(vdone, v.n)
                    v.up(dve.tensor_copy(bucket[:, :], work_i[:, :]))
                    if way == 0:
                        dve.wait_ge(vdone, v.n)
                        v.up(dve.tensor_scalar(work_i[:, :], key[:, :], P - 1, None, ALU.bitwise_and))
                        dve.wait_ge(vdone, v.n)
                        v.up(dve.tensor_copy(recs[way][:, :, 1], work_i[:, :]))
                    else:
                        v.up(dve.tensor_copy(recs[way][:, :, 2], key[:, :]))
                    n = v.n
                    with dve.Fori(0, NT) as b:
                        dve.wait_ge(vdone, b + n)
                        dve.tensor_scalar(inside[:, :], bucket[:, :], iota[0:EDGE_ROWS, bass.ds(b, 1)], None,
                                          ALU.is_equal, ALU.add, accum_out=count[:, bass.ds(b, 1)]).then_inc(vdone, 1)
                    v.n += NT
                    dve.wait_ge(vdone, v.n)
                    dve.sem_inc(counted[way], 1)
                    dve.wait_ge(count_summed[way], 1)
                    v.up(dve.memset(place[:, :], 1.0))
                    if way == 0:
                        end_buckets(way, SIZE_M)
                        v.up(dve.tensor_sub(base[:, :], tend[:, :], groups[:, :]))
                        dve.wait_ge(vdone, v.n)
                        v.up(dve.scalar_tensor_tensor(base[:, :], base[:, :], float(SIZE_M), ps_count[:, way, 1, :], ALU.mult, ALU.add))
                    else:
                        dve.wait_ge(vdone, v.n)
                        v.up(dve.tensor_scalar(groups[:, :], ps_count[:, way, 0, :], 1.0, None, ALU.mult))
                        dve.wait_ge(vdone, v.n)
                        v.up(dve.tensor_tensor_scan(base[:, :], groups[:, :], nil_t[:, :], 0.0, ALU.add, ALU.add))
                        dve.wait_ge(vdone, v.n)
                        v.up(dve.tensor_sub(base[:, :], base[:, :], groups[:, :]))
                        dve.wait_ge(vdone, v.n)
                        v.up(dve.tensor_tensor(base[:, :], base[:, :], ps_count[:, way, 1, :], ALU.add))
                    parts = (slice(0, HEAD), slice(HEAD, EC)) if way == 0 else (slice(0, EC),)
                    for part in parts:
                        width = part.stop - part.start
                        n = v.n
                        with dve.Fori(0, NT) as b:
                            begin = base[0:EDGE_ROWS, bass.ds(b, 1)]
                            rises = in_register(dve, b * 3 + n)
                            dve.wait_ge(vdone, rises)
                            dve.tensor_scalar(inside[:, part], bucket[:, part], iota[0:EDGE_ROWS, bass.ds(b, 1)], None,
                                              ALU.is_equal).then_inc(vdone, 1)
                            dve.wait_ge(vdone, rises + 1)
                            dve.tensor_tensor_scan(ranks[:, part], inside[:, part], nil[:, 0:1].to_broadcast([EDGE_ROWS, width]),
                                                   begin, ALU.add, ALU.add).then_inc(vdone, 1)
                            dve.wait_ge(vdone, rises + 2)
                            if part.stop < EC:
                                dve.tensor_scalar(begin, ranks[:, part.stop - 1:part.stop], 1.0, None, ALU.mult)
                            else:
                                dve.nop(nofuse=True)
                            dve.copy_predicated(place[:, part], inside[:, part], ranks[:, part]).then_inc(vdone, 1)
                        v.n += 3 * NT
                        dve.wait_ge(vdone, v.n)
                        if way == 0:
                            v.up(dve.tensor_scalar(work_i[:, part], place[:, part], -1.0, None, ALU.add))
                            dve.wait_ge(vdone, v.n)
                            v.up(dve.tensor_scalar(ranks[:, part].bitcast(I32), work_i[:, part], P - 1, None, ALU.bitwise_and))
                            v.up(dve.tensor_scalar(place[:, part].bitcast(I32), work_i[:, part], 7, None, ALU.logical_shift_right))
                            dve.wait_ge(vdone, v.n)
                            v.up(dve.scalar_tensor_tensor(addr[way][:, part], ranks[:, part].bitcast(I32), float(T_M),
                                                          place[:, part].bitcast(I32), ALU.mult, ALU.add))
                            if part.start == 0:
                                v.up(dve.scalar_tensor_tensor(recs[way][:, :, 0], other[:, :], float(R), type_i[:, :], ALU.mult, ALU.add))
                        else:
                            v.up(dve.tensor_scalar(addr[way][:, :], place[:, :], -1.0, None, ALU.add))
                            v.up(dve.scalar_tensor_tensor(recs[way][:, :, 0], other[:, :], float(R), type_i[:, :], ALU.mult, ALU.add))
                            v.up(dve.tensor_copy(recs[way][:, :, 1], other[:, :]))
                            v.up(dve.tensor_tensor(ranks[:, :], place[:, :], edge_i[:, :], ALU.not_equal))
                            dve.wait_ge(vdone, v.n)
                            v.up(dve.tensor_reduce(astray[:, :], ranks[:, :], AX.X, ALU.add))
                            dve.wait_ge(vdone, v.n)
                            dve.sem_inc(astray_found, 1)
                        dve.wait_ge(vdone, v.n)
                        dve.sem_inc(placed[way], 1)
                    if way == 0:
                        find_owners(group_f[0], GC_M, owner_i[0])
                    else:
                        for kind, size, columns in ((0, SIZE_M, GC_M), (1, SIZE, GC)):
                            end_buckets(way, size)
                            find_owners(group_f[kind], columns, owner_i[1 + kind])
                            find_starts(way, size, group_f[kind], columns, first[kind], start_i[kind])
                        dve.wait_ge(astray_summed, 1)
                        dve.tensor_copy(astray_i[:, :], ps_astray[0:1, :]).then_inc(astray_known, 1)
                    dve.wait_ge(vdone, v.n)
                    dve.sem_inc(owner_made, 1)
                    if way == 0:
                        n = v.n
                        with dve.Fori(0, EDGE_STEPS) as step:
                            for half in range(2):
                                dve.wait_ge(feat_landed[half], step * 16 + 16)
                                dve.tensor_tensor(feat[:, half, :, :], feat[:, half, :, :],
                                                  a_edge[:, :].unsqueeze(1).to_broadcast([EDGE_ROWS, CHUNK, ED]),
                                                  ALU.mult).then_inc(vdone, 1)
                                dve.wait_ge(vdone, step * 2 + (n + half + 1))
                                dve.tensor_reduce(recs[1][:, bass.ds(step * 2 * CHUNK + half * CHUNK, CHUNK), 3],
                                                  feat[:, half, :, :], AX.X, ALU.add).then_inc(feat_used, 1)
                        v.n += 2 * EDGE_STEPS
                        dve.wait_ge(feat_used, 2 * EDGE_STEPS)
                        dve.sem_inc(features_dotted, 1)

            @block.tensor
            def _(pe):
                def sum_counts(way):
                    pe.wait_ge(counted[way], 1)
                    nc.tensor.matmul(ps_count[:, way, 0, :], ones[:, :], count[:, :], start=True, stop=True)
                    nc.tensor.matmul(ps_count[:, way, 1, :], below[:, :], count[:, :], start=True, stop=True)\
                        .then_inc(count_summed[way], 1)

                def project(way, pair, buf):
                    t = pair * 2 + (way * NT + buf)
                    seen = (NT + 1 - buf) // 2 * way + 1
                    pe.wait_ge(xT_landed[buf], pair * 16 + seen * 16)
                    for g in range(2 * BLOCKS):
                        pe.wait_ge(proj_copied, t * (2 * BLOCKS) + (g + 1))
                        for k in range(KC):
                            r0 = g * 512 // D
                            last = nc.tensor.matmul(ps_proj[:, g % BANKS, :], xT[:, buf, k, :],
                                                    w_rel[:, k, r0:r0 + 512 // D, :], start=(k == 0), stop=(k == KC - 1))
                        last.then_inc(proj_summed, 1)

                for way in range(2):
                    sum_counts(way)
                    pe.wait_ge(w_landed, 16 * KC * (way + 1))
                    with pe.Fori(0, PAIRS) as pair:
                        project(way, pair, 0)
                        project(way, pair, 1)
                    for t in range(2 * PAIRS, NT):
                        project(way, t // 2, t % 2)
                pe.wait_ge(astray_found, 1)
                nc.tensor.matmul(ps_astray[:, :], ones[:, :], astray[:, :], start=True, stop=True).then_inc(astray_summed, 1)

            @block.scalar
            def _(act):
                act.sem_inc(proj_copied, BANKS)
                for way, w, table in ((0, Wb, table_b), (1, Wf, table_f)):
                    if way:
                        act.wait_ge(proj_summed, NT * 2 * BLOCKS)
                    for k in range(KC):
                        act.dma_start(w_rel[:, k, :, :], w[:, k * P:(k + 1) * P, :].rearrange("r i o -> i r o"))\
                            .then_inc(w_landed, 16)

                    def load_x(pair, buf):
                        act.dma_start(xT[:, buf, :, :], xT_pad[:, bass.ds(pair * 2 * P + buf * P, P)].rearrange("(k p) n -> p k n", p=P))\
                            .then_inc(xT_landed[buf], 16)

                    def tile(pair, buf, first, last):
                        t = pair * 2 + (way * NT + buf)
                        if not last:
                            load_x(pair + buf, 1 - buf)
                        for half in range(2):
                            if not first:
                                act.wait_ge(proj_stored[half], t * 16)
                            for g in range(half * BLOCKS, (half + 1) * BLOCKS):
                                act.wait_ge(proj_summed, t * (2 * BLOCKS) + (g + 1))
                                act.activation(proj[:, half, (g % BLOCKS) * 512:(g % BLOCKS + 1) * 512],
                                               ps_proj[:, g % BANKS, :], ACT.Copy).then_inc(proj_copied, 1)
                            act.wait_ge(proj_copied, t * (2 * BLOCKS) + ((half + 1) * BLOCKS + BANKS))
                            act.dma_start(table.ap()[bass.ds(pair * 2 * P + buf * P, P), half * HALF_W:(half + 1) * HALF_W],
                                          proj[:, half, :]).then_inc(proj_stored[half], 16)

                    load_x(0, 0)
                    tile(0, 0, way == 0, False)
                    tile(0, 1, False, False)
                    with act.Fori(1, PAIRS) as pair:
                        tile(pair, 0, False, False)
                        tile(pair, 1, False, False)
                    for t in range(2 * PAIRS, NT):
                        tile(t // 2, t % 2, False, t == NT - 1)
                for half in range(2):
                    act.wait_ge(proj_stored[half], 2 * NT * 16)
                act.wait_ge(owner_made, 2)
                for table, columns, here in ((owner_b, GC_M, owner_i[0]), (owner_m, GC_M, owner_i[1]), (owner_a, GC, owner_i[2]),
                                             (start_m, GC_M, start_i[0]), (start_a, GC, start_i[1]),
                                             (first_m, GC_M, first[0]), (first_a, GC, first[1])):
                    act.dma_start(table.ap().rearrange("(p c) -> p c", c=columns), here[:, :]).then_inc(owner_stored, 16)

        slots_sb_a = sb("slots_sb_a", [P, T, 4])
        owner_sb_a = sb("owner_sb_a", [1, P * GC], I32)
        acc_b = sb("acc_b", [P, NT * ROW])
        acc_f = sb("acc_f", [P, NT * ROW])
        rows_b = acc_b[:, :].rearrange("p (t w) -> p t w", w=ROW)
        rows_f = acc_f[:, :].rearrange("p (t w) -> p t w", w=ROW)

        def in_pairs(eng, stages):
            def steps(numbers):
                for i in numbers:
                    for stage, lag in stages:
                        if 0 <= i - lag < NT:
                            stage(i - lag, (i - lag) // 2, (i - lag) % 2)

            steps(range(2))
            with eng.Fori(1, PAIRS) as pair:
                for q in range(2):
                    for stage, lag in stages:
                        stage(pair * 2 + (q - lag), pair + (q - lag) // 2, (q - lag) % 2)
            steps(range(2 * PAIRS, NT + max(lag for _, lag in stages)))

        with ExitStack() as two:
            index = sb("index", [P, RING, GROUP], U32, two)
            local = sb("local", [P, RING, GROUP, 2], scope=two)
            first_sb_a = sb("first_sb_a", [P, GROUPS], scope=two)
            messages = ExitStack()
            gathered = sb("gathered", [P, RING, GROUP_M, ROW], scope=messages)
            slots_sb_b = sb("slots_sb_b", [P, T_M, 2], scope=messages)
            slots_sb_m = sb("slots_sb_m", [P, T_M, 4], scope=messages)
            owner_sb = [sb("owner_sb_b", [1, P * GC_M], I32, messages), sb("owner_sb_m", [1, P * GC_M], I32, messages)]
            start_sb = sb("start_sb", [1, P * GC_M], I32, messages)
            slots_landed = sem("slots_landed")
            groups_landed = sem("groups_landed")
            first_landed = sem("first_landed")
            local_made = sem("local_made")

            def ring_of_sems(name):
                return [sem(f"{name}{q}") for q in range(RING)]

            cleared = sem("cleared")
            staged = ring_of_sems("staged")
            landed = ring_of_sems("landed")
            matched = ring_of_sems("matched")
            summed = ring_of_sems("summed")
            added = ring_of_sems("added")

            def add_messages(way, slots_sb, table, acc):
                tiles, turns = GROUP_M, TURNS_M
                turn0 = TURNS_BEFORE[way]
                with ExitStack() as scope:
                    name = "bf"[way]
                    match = sb("match_" + name, [P, RING, tiles, P], scope=scope)
                    if way == 1:
                        first_sb = sb("first_sb", [P, GROUPS_M], scope=scope)
                    ps_sum = psum("ps_sum_" + name, [P, RING, 512], scope)
                    block = scope.enter_context(nc.Block())

                    @block.sync
                    def _(sp):
                        def load_groups(turns, tiles, slots_sb):
                            with sp.Fori(0, turns) as turn:
                                for q in range(RING):
                                    e0 = sp.value_load(start_sb[0:1, bass.ds(turn * RING + q, 1)], min_val=0, max_val=E)
                                    sp.dma_start(slots_sb[:, bass.ds(turn * (RING * tiles) + q * tiles, tiles), :],
                                                 sorted_f.ap()[bass.ds(e0, tiles * P), :].rearrange("(p u) w -> p u w", u=tiles))\
                                        .then_inc(groups_landed, 16)

                        if way == 0:
                            sp.dma_start(slots_sb_b[:, :, :], slots_b.ap().rearrange("(p t) w -> p t w", t=T_M)).then_inc(slots_landed, 16)
                            for per_group, there in ((owner_b, owner_sb[0]), (owner_m, owner_sb[1]), (start_m, start_sb)):
                                sp.dma_start(there[:, :], per_group.ap().rearrange("(a t) -> a t", a=1)).then_inc(slots_landed, 16)
                            sp.wait_ge(slots_landed, 64)
                            load_groups(TURNS_M, GROUP_M, slots_sb_m)
                            sp.wait_ge(groups_landed, 16 * GROUPS_M)
                        else:
                            sp.dma_start(first_sb[:, :], first_m.ap()[0:GROUPS_M].rearrange("(a t) -> a t", a=1).to_broadcast([P, GROUPS_M]))\
                                .then_inc(first_landed, 16)
                            sp.dma_start(first_sb_a[:, :], first_a.ap()[0:GROUPS].rearrange("(a t) -> a t", a=1).to_broadcast([P, GROUPS]))\
                                .then_inc(first_landed, 16)
                            sp.dma_start(owner_sb_a[:, :], owner_a.ap().rearrange("(a t) -> a t", a=1)).then_inc(slots_landed, 16)
                            sp.dma_start(start_sb[:, 0:P * GC], start_a.ap().rearrange("(a t) -> a t", a=1)).then_inc(slots_landed, 16)
                            sp.wait_ge(slots_landed, 96)
                            load_groups(TURNS, GROUP, slots_sb_a)
                            sp.wait_ge(groups_landed, 16 * (GROUPS_M + GROUPS))

                    @block.scalar
                    def _(act):
                        if way == 0:
                            for q in range(RING):
                                act.sem_inc(summed[q], 1)
                        act.wait_ge(slots_landed, 64)
                        if way == 1:
                            act.wait_ge(local_made, 1)
                        with act.Fori(turn0, turn0 + turns) as turn:
                            for q in range(RING):
                                act.wait_ge(summed[q], turn + 1)
                                there = bass.ds((turn - turn0) * (RING * tiles) + q * tiles, tiles)
                                act.activation(index[:, q, 0:tiles], slots_sb[:, there, 0], ACT.Copy)
                                act.activation(local[:, q, 0:tiles, 0], slots_sb[:, there, way + 1], ACT.Copy).then_inc(staged[q], 1)

                    @block.gpsimd
                    def _(pool):
                        pool.wait_ge(cleared, way * 2 + 2)
                        with pool.Fori(turn0, turn0 + turns) as turn:
                            for q in range(RING):
                                pool.wait_ge(staged[q], turn + 1)
                                pool.nop(nofuse=True)
                                for u in range(tiles):
                                    pool.indirect_dma_start(
                                        gathered[:, q, u, 0:D], None, table,
                                        bass.IndirectOffsetOnAxis(ap=index[:, q, u:u + 1], axis=0)).then_inc(landed[q], 16)
                        for q in range(RING):
                            pool.wait_ge(landed[q], LANDED_BEFORE[way + 1])

                    @block.vector
                    def _(dve):
                        dve.memset(acc[:, :], 0.0).then_inc(cleared, 1)
                        dve.memset(gathered[:, :, :, COUNT], 1.0).then_inc(cleared, 1)
                        dve.wait_ge(cleared, way * 2 + 2)
                        dve.wait_ge(slots_landed, 64)
                        if way == 1:
                            dve.wait_ge(first_landed, 32)
                            nodes = slots_sb_m[:, :, 2].rearrange("p (g u) -> p g u", u=GROUP_M)
                            dve.tensor_tensor(nodes, nodes, first_sb[:, :].unsqueeze(2).to_broadcast([P, GROUPS_M, GROUP_M]),
                                              ALU.subtract).then_inc(local_made, 1)
                        else:
                            for q in range(RING):
                                dve.sem_inc(added[q], 1)

                        def match_group(turn, q):
                            dve.wait_ge(staged[q], turn + 1)
                            for u in range(tiles):
                                last = dve.tensor_scalar(match[:, q, u, :], iota[:, :], local[:, q, u, 0:1], None, ALU.is_equal)
                            last.then_inc(matched[q], 1)

                        def add(turn, q):
                            at = dve.value_load(owner_sb[way][0:1, bass.ds((turn - turn0) * RING + q, 1)],
                                                min_val=0, max_val=(NT - 1) * ROW)
                            if q:
                                dve.wait_ge(added[q - 1], turn + 2)
                            else:
                                dve.wait_ge(added[RING - 1], turn + 1)
                            dve.wait_ge(summed[q], turn + 2)
                            dve.tensor_tensor(acc[:, bass.ds(at, COUNT + 1)], acc[:, bass.ds(at, COUNT + 1)],
                                              ps_sum[:, q, 0:COUNT + 1], ALU.add).then_inc(added[q], 1)

                        with dve.Fori(turn0, turn0 + turns) as turn:
                            match_group(turn, 0)
                            for q in range(1, RING):
                                match_group(turn, q)
                                add(turn, q - 1)
                            add(turn, RING - 1)

                    @block.tensor
                    def _(pe):
                        with pe.Fori(turn0, turn0 + turns) as turn:
                            for q in range(RING):
                                pe.wait_ge(landed[q], turn * (16 * tiles) + (LANDED_BEFORE[way] + (1 - turn0) * 16 * tiles))
                                pe.wait_ge(matched[q], turn + 1)
                                pe.wait_ge(added[q], turn + 1)
                                for u in range(tiles):
                                    last = nc.tensor.matmul(ps_sum[:, q, 0:COUNT + 1], match[:, q, u, :],
                                                            gathered[:, q, u, 0:COUNT + 1],
                                                            start=(u == 0), stop=(u == tiles - 1))
                                last.then_inc(summed[q], 1)

            add_messages(0, slots_sb_b, table_b.ap().rearrange("n (r d) -> (n r) d", d=D), acc_b)
            add_messages(1, slots_sb_m, table_f.ap().rearrange("n (r d) -> (n r) d", d=D), acc_f)
            messages.close()

            with ExitStack() as three:
                def s3(name, shape, dt=F32):
                    return sb(name, shape, dt, three)

                x_rows = s3("x_rows", [P, 2, D])
                x_cols = s3("x_cols", [P, 2, KC, P])
                w_loop = s3("w_loop", [P, KC, D])
                bias = [s3("bias_b", [P, D]), s3("bias_f", [P, D]), s3("bias_s", [P, D])]
                w_att = s3("w_att", [P, KC, D])
                a_att = s3("a_att", [P, KC, 2])
                w_z = s3("w_z", [P, KC, D + 2])
                inv = [s3("inv_b", [P, NT]), s3("inv_f", [P, NT])]
                some = [s3("some_b", [P, NT]), s3("some_f", [P, NT])]
                h = s3("h", [P, D])
                fresh = s3("fresh", [P, ROW])
                stats = s3("stats", [P, 6])
                moments = s3("moments", [P, 2])
                eps = s3("eps", [P, 1])
                spread = s3("spread", [P, 1])
                x1 = s3("x1", [P, D])
                x1T = s3("x1T", [P, KC, P])
                z_row = s3("z_row", [P, 2, DENOM + 1])
                ps_loop = psum("ps_loop", [P, 2, 512], three)[:, :, 0:D]
                ps_u = psum("ps_u", [P, 512], three)[:, 0:2 * KC].rearrange("p (k j) -> p k j", j=2)
                ps_t = psum("ps_t", [P, 512], three)[:, 0:D].rearrange("p (k n) -> p k n", n=P)
                ps_z = psum("ps_z", [P, 512], three)[:, 0:D + 2]
                weights_landed = sem("weights_landed")
                x_landed = [sem("x_landed0"), sem("x_landed1")]
                vnorm = sem("vnorm")
                u_summed = sem("u_summed")
                looped = sem("looped")
                std_made = sem("std_made")
                x1_made = sem("x1_made")
                x1_turned = sem("x1_turned")
                x1T_made = sem("x1T_made")
                z_summed = sem("z_summed")
                z_made = sem("z_made")
                z_stored = [sem("z_stored0"), sem("z_stored1")]
                block = three.enter_context(nc.Block())
                STEPS = 10
                PRE = 12

                @block.sync
                def _(sp):
                    for k in range(KC):
                        rows = slice(k * P, (k + 1) * P)
                        sp.dma_start(w_loop[:, k, :], loop_weight[rows, :]).then_inc(weights_landed, 16)
                        sp.dma_start(w_att[:, k, :], W1[rows, :]).then_inc(weights_landed, 16)
                        sp.dma_start(w_z[:, k, 0:D], W1T[rows, :]).then_inc(weights_landed, 16)
                        for j in range(2):
                            sp.dma_start(a_att[:, k, j:j + 1], A1[0:1, j * D + k * P:j * D + (k + 1) * P].rearrange("a p -> p a"))\
                                .then_inc(weights_landed, 16)
                    for b, vec in zip(bias, (backward_bias, forward_bias, self_bias)):
                        sp.dma_start(b[:, :], vec.rearrange("(a n) -> a n", a=1).to_broadcast([P, D])).then_inc(weights_landed, 16)

                    def store(t, pair, buf):
                        sp.wait_ge(z_made, t + 1)
                        sp.dma_start(z_table.ap()[bass.ds(t * P, P), :], z_row[:, buf, :]).then_inc(z_stored[buf], 16)

                    in_pairs(sp, [(store, 0)])
                    for buf in range(2):
                        sp.wait_ge(z_stored[buf], ((NT + 1 - buf) // 2 + 1) * 16)

                @block.gpsimd
                def _(pool):
                    def load(t, pair, buf):
                        if not isinstance(t, int) or t >= 2:
                            pool.wait_ge(vnorm, t * STEPS + (PRE + 3 - 2 * STEPS))
                        pool.dma_start(x_rows[:, buf, :], x_pad[bass.ds(t * P, P), :]).then_inc(x_landed[buf], 16)
                        pool.dma_start(x_cols[:, buf, :, :], xT_pad[:, bass.ds(t * P, P)].rearrange("(k p) n -> p k n", p=P))\
                            .then_inc(x_landed[buf], 16)

                    in_pairs(pool, [(load, 0)])

                @block.tensor
                def _(pe):
                    pe.wait_ge(weights_landed, 16 * (5 * KC + 3))
                    for k in range(KC):
                        for j in range(KC):
                            last = nc.tensor.matmul(ps_u[:, k, :], w_att[:, j, k * P:(k + 1) * P], a_att[:, j, :],
                                                    start=(j == 0), stop=(j == KC - 1))
                    last.then_inc(u_summed, 1)

                    def loop_product(t, pair, buf):
                        pe.wait_ge(x_landed[buf], pair * 32 + 32)
                        for k in range(KC):
                            last = nc.tensor.matmul(ps_loop[:, buf, :], x_cols[:, buf, k, :], w_loop[:, k, :],
                                                    start=(k == 0), stop=(k == KC - 1))
                        last.then_inc(looped, 1)

                    def make_z(t, pair, buf):
                        pe.wait_ge(x1_made, t + 1)
                        for k in range(KC):
                            last = nc.tensor.transpose(ps_t[:, k, :], x1[:, k * P:(k + 1) * P], ident[:, :])
                        last.then_inc(x1_turned, 1)
                        pe.wait_ge(x1T_made, t + 1)
                        for k in range(KC):
                            last = nc.tensor.matmul(ps_z[:, :], x1T[:, k, :], w_z[:, k, :],
                                                    start=(k == 0), stop=(k == KC - 1))
                        last.then_inc(z_summed, 1)

                    in_pairs(pe, [(make_z, 2), (loop_product, 0)])

                @block.scalar
                def _(act):
                    for buf in range(2):
                        act.sem_inc(z_stored[buf], 16)

                    def make_std(t, pair, buf):
                        act.wait_ge(vnorm, t * STEPS + (PRE + 8))
                        act.activation(spread[:, :], moments[:, 1:2], ACT.Sqrt, bias=eps[:, 0:1]).then_inc(std_made, 1)

                    def copy_z(t, pair, buf):
                        act.wait_ge(x1_turned, t + 1)
                        act.activation(x1T[:, :, :], ps_t[:, :, :], ACT.Copy).then_inc(x1T_made, 1)
                        act.activation(acc_f[:, bass.ds(t * ROW, D)], x1[:, :], ACT.Copy)
                        act.wait_ge(z_stored[buf], pair * 16 + 16)
                        act.wait_ge(z_summed, t + 1)
                        act.activation(z_row[:, buf, 0:COUNT + 1], ps_z[:, 0:COUNT + 1], ACT.Copy).then_inc(z_made, 1)

                    in_pairs(act, [(copy_z, 2), (make_std, 1)])

                @block.vector
                def _(dve):
                    v = Tally(vnorm)
                    v.up(dve.memset(eps[:, :], EPS))
                    v.up(dve.memset(z_row[:, :, DENOM:DENOM + 1], 1.0))
                    for way, rows in ((0, rows_b), (1, rows_f)):
                        v.up(dve.tensor_scalar(inv[way][:, :], rows[:, :, COUNT], 1.0, None, ALU.max))
                        dve.wait_ge(vnorm, v.n)
                        v.up(dve.reciprocal(inv[way][:, :], inv[way][:, :]))
                        v.up(dve.tensor_scalar(some[way][:, :], rows[:, :, COUNT], 1.0, None, ALU.min))
                    dve.wait_ge(weights_landed, 16 * (5 * KC + 3))
                    dve.wait_ge(u_summed, 1)
                    for k in range(KC):
                        v.up(dve.tensor_copy(w_z[:, k, D:D + 2], ps_u[:, k, :]))
                    v.up(dve.memset(fresh[:, 0:NEG_MAX], 0.0))
                    v.up(dve.memset(fresh[:, NEG_MAX:ROW], FLOOR))
                    assert v.n == PRE

                    def add_up(t, pair, buf):
                        at = in_register(dve, t * ROW)
                        rises = in_register(dve, t * STEPS + PRE)
                        sums_b, sums_f = acc_b[:, bass.ds(at, D)], acc_f[:, bass.ds(at, D)]

                        def step(k):
                            dve.wait_ge(vnorm, rises + k)

                        dve.wait_ge(x_landed[buf], pair * 32 + 32)
                        if not isinstance(t, int) or t:
                            dve.wait_ge(x1_made, t)
                        step(0)
                        dve.scalar_tensor_tensor(h[:, :], sums_f, inv[1][:, bass.ds(t, 1)], x_rows[:, buf, :], ALU.mult, ALU.add).then_inc(vnorm, 1)
                        step(1)
                        dve.scalar_tensor_tensor(h[:, :], sums_b, inv[0][:, bass.ds(t, 1)], h[:, :], ALU.mult, ALU.add).then_inc(vnorm, 1)
                        dve.wait_ge(looped, t + 1)
                        step(2)
                        dve.scalar_tensor_tensor(h[:, :], ps_loop[:, buf, :], 2.0, h[:, :], ALU.mult, ALU.add).then_inc(vnorm, 1)
                        for k, way in ((3, 0), (4, 1)):
                            step(k)
                            dve.scalar_tensor_tensor(h[:, :], bias[way][:, :], some[way][:, bass.ds(t, 1)], h[:, :],
                                                     ALU.mult, ALU.add).then_inc(vnorm, 1)
                        step(5)
                        dve.tensor_tensor(h[:, :], h[:, :], bias[2][:, :], ALU.add).then_inc(vnorm, 1)
                        step(6)
                        dve.bn_stats(stats[:, :], h[:, :]).then_inc(vnorm, 1)
                        step(7)
                        dve.nop(nofuse=True)
                        dve.bn_aggr(moments[:, :], stats[:, :]).then_inc(vnorm, 1)
                        dve.tensor_scalar(acc_b[:, bass.ds(at, NEG_MAX)], fresh[:, 0:NEG_MAX], 1.0, None, ALU.mult).then_inc(vnorm, 1)

                    def norm(t, pair, buf):
                        dve.wait_ge(std_made, t + 1)
                        dve.reciprocal(spread[:, :], spread[:, :]).then_inc(vnorm, 1)
                        dve.wait_ge(vnorm, t * STEPS + (PRE + STEPS))
                        dve.tensor_scalar(x1[:, :], h[:, :], moments[:, 0:1], spread[:, 0:1], ALU.subtract, ALU.mult)\
                            .then_inc(x1_made, 1)

                    def keep_dst(t, pair, buf):
                        dve.wait_ge(z_made, t + 1)
                        dve.tensor_scalar(acc_b[:, bass.ds(t * ROW + S_DST, 1)], ps_z[:, D + 1:D + 2], 1.0, None, ALU.mult)
                        dve.tensor_scalar(acc_b[:, bass.ds(t * ROW + NEG_MAX, 1)], fresh[:, NEG_MAX:ROW - 1], 1.0, None, ALU.mult)

                    in_pairs(dve, [(norm, 2), (add_up, 1), (keep_dst, 2)])

            with ExitStack() as four:
                def s4(name, shape, dt=F32):
                    return sb(name, shape, dt, four)

                spread_e = s4("spread_e", [P, RING, GROUP, P])
                gathered = s4("gathered_z", [P, RING, GROUP, ROW])
                raw = s4("raw", [P, 2, SIZE])
                logit = s4("logit", [P, 2, SIZE])
                prob = s4("prob", [P, 2, GROUP, P])
                probT = s4("probT", [P, 2, SIZE])
                v_edge = s4("v_edge", [P, RING, GROUP])
                s_dst = s4("s_dst", [P, RING])
                top = s4("top", [P, RING])
                neg_max = s4("neg_max", [P, RING])
                drop = s4("drop", [P, RING])
                shrink = s4("shrink", [P, RING])
                ps_v = psum("ps_v", [P, 2, 512], four)
                ps_p = psum("ps_p", [P, 2, 512], four)
                ps_o = psum("ps_o", [P, RING // 2, 512], four)
                v_made = ring_of_sems("v_made")
                spread_made = ring_of_sems("spread_made")
                v_turned = ring_of_sems("v_turned")
                raw_made = ring_of_sems("raw_made")
                logit_made = ring_of_sems("logit_made")
                top_made = ring_of_sems("top_made")
                lowered = ring_of_sems("lowered")
                dropped = ring_of_sems("dropped")
                maxed = ring_of_sems("maxed")
                prob_made = ring_of_sems("prob_made")
                prob_turned = ring_of_sems("prob_turned")
                probT_made = ring_of_sems("probT_made")
                turn0 = TURNS_BEFORE[2]
                block = four.enter_context(nc.Block())

                def staggered(eng, stages, begin=lambda: None):
                    for q in range(RING):
                        for stage, lag in stages:
                            if q >= lag:
                                stage(0, q - lag)
                    with eng.Fori(1, TURNS) as turn:
                        begin()
                        for q in range(RING):
                            for stage, lag in stages:
                                if q >= lag:
                                    stage(turn, q - lag)
                                else:
                                    stage(turn - 1, q - lag + RING)
                    begin()
                    for q in range(max(lag for _, lag in stages)):
                        for stage, lag in stages:
                            if q < lag:
                                stage(TURNS - 1, q - lag + RING)

                @block.gpsimd
                def _(pool):
                    with pool.Fori(0, TURNS) as turn:
                        for q in range(RING):
                            pool.wait_ge(staged[q], turn + (turn0 + 1))
                            pool.nop(nofuse=True)
                            for u in range(GROUP):
                                pool.indirect_dma_start(
                                    gathered[:, q, u, 0:DENOM + 1], None, z_table.ap(),
                                    bass.IndirectOffsetOnAxis(ap=index[:, q, u:u + 1], axis=0)).then_inc(landed[q], 16)
                    for q in range(RING):
                        pool.wait_ge(landed[q], LANDED_BEFORE[2] + TURNS * GROUP * 16)

                @block.scalar
                def _(act):
                    for q in range(RING):
                        act.sem_inc(probT_made[q], 1)

                    act.wait_ge(local_made, 2)

                    def stage(turn, q):
                        act.wait_ge(summed[q], turn + (turn0 + 1))
                        there = bass.ds(turn * (RING * GROUP) + q * GROUP, GROUP)
                        act.activation(index[:, q, :], slots_sb_a[:, there, 1], ACT.Copy)
                        act.activation(local[:, q, :, :], slots_sb_a[:, there, 2:4], ACT.Copy).then_inc(staged[q], 1)
                        at = act.value_load(owner_sb_a[0:1, bass.ds(turn * RING + q, 1)], min_val=0, max_val=(NT - 1) * ROW)
                        act.activation(s_dst[:, q:q + 1], acc_b[:, bass.ds(at + S_DST, 1)], ACT.Copy)

                    def add_v(turn, q):
                        act.wait_ge(v_made[q], turn + 1)
                        for u in range(GROUP):
                            last = act.activation(spread_e[:, q, u, :], spread_e[:, q, u, :], ACT.Identity,
                                                  bias=v_edge[:, q, u:u + 1])
                        last.then_inc(spread_made[q], 1)

                    def add_dst(turn, q):
                        act.wait_ge(v_turned[q], turn + 1)
                        act.activation(raw[:, q % 2, :], ps_v[:, q % 2, :], ACT.Identity,
                                       bias=s_dst[:, q:q + 1]).then_inc(raw_made[q], 1)

                    def to_prob(turn, q):
                        act.wait_ge(maxed[q], turn + 1)
                        act.activation(prob[:, q % 2, :, :].rearrange("p u e -> p (u e)"), logit[:, q % 2, :], ACT.Exp,
                                       bias=neg_max[:, q:q + 1])
                        act.activation(shrink[:, q:q + 1], drop[:, q:q + 1], ACT.Exp).then_inc(prob_made[q], 1)

                    def copy_probT(turn, q):
                        act.wait_ge(prob_turned[q], turn + 1)
                        act.activation(probT[:, q % 2, :], ps_p[:, q % 2, :], ACT.Copy).then_inc(probT_made[q], 1)

                    staggered(act, [(add_v, 4), (to_prob, 5), (add_dst, 4), (stage, 0), (copy_probT, 5)])

                @block.vector
                def _(dve):
                    nodes = slots_sb_a[:, :, 2].rearrange("p (g u) -> p g u", u=GROUP)
                    dve.tensor_tensor(nodes, nodes, first_sb_a[:, :].unsqueeze(2).to_broadcast([P, GROUPS, GROUP]),
                                      ALU.subtract).then_inc(local_made, 1)
                    kept = {}

                    def owner_of(turn, q):
                        return dve.value_load(owner_sb_a[0:1, bass.ds(turn * RING + q, 1)], min_val=0, max_val=(NT - 1) * ROW)

                    def mask(turn, q):
                        dve.wait_ge(staged[q], turn + (turn0 + 1))
                        for u in range(GROUP):
                            dve.tensor_scalar(spread_e[:, q, u, :], iota[:, :], local[:, q, u, 0:1], -FAR,
                                              ALU.not_equal, ALU.mult)

                    def make_v(turn, q):
                        dve.wait_ge(landed[q], turn * (16 * GROUP) + (LANDED_BEFORE[2] + 16 * GROUP))
                        dve.tensor_tensor(v_edge[:, q, :], gathered[:, q, :, D], local[:, q, :, 1], ALU.add).then_inc(v_made[q], 1)

                    def new_max(turn, q):
                        at = kept[q] = owner_of(turn, q)
                        old = acc_b[:, bass.ds(at + NEG_MAX, 1)]
                        dve.wait_ge(raw_made[q], turn + 1)
                        dve.scalar_tensor_tensor(logit[:, q % 2, :], raw[:, q % 2, :], ALPHA, raw[:, q % 2, :],
                                                 ALU.mult, ALU.max).then_inc(logit_made[q], 1)
                        dve.wait_ge(logit_made[q], turn + 1)
                        dve.tensor_reduce(top[:, q:q + 1], logit[:, q % 2, :], AX.X, ALU.max).then_inc(top_made[q], 1)
                        dve.wait_ge(top_made[q], turn + 1)
                        if q:
                            dve.wait_ge(maxed[q - 1], turn + 1)
                        elif not isinstance(turn, int) or turn:
                            dve.wait_ge(maxed[RING - 1], turn)
                        dve.scalar_tensor_tensor(neg_max[:, q:q + 1], top[:, q:q + 1], -1.0, old, ALU.mult, ALU.min)\
                            .then_inc(lowered[q], 1)
                        dve.wait_ge(lowered[q], turn + 1)
                        dve.tensor_tensor(drop[:, q:q + 1], neg_max[:, q:q + 1], old, ALU.subtract).then_inc(dropped[q], 1)
                        dve.wait_ge(dropped[q], turn + 1)
                        dve.tensor_scalar(old, neg_max[:, q:q + 1], 1.0, None, ALU.mult).then_inc(maxed[q], 1)

                    def add(turn, q):
                        at = kept.pop(q) if q in kept else owner_of(turn, q)
                        sums = acc_b[:, bass.ds(at, DENOM + 1)]
                        if q:
                            dve.wait_ge(added[q - 1], turn + (turn0 + 2))
                        else:
                            dve.wait_ge(added[RING - 1], turn + (turn0 + 1))
                        dve.wait_ge(summed[q], turn + (turn0 + 2))
                        dve.scalar_tensor_tensor(sums, sums, shrink[:, q:q + 1], ps_o[:, q % (RING // 2), 0:DENOM + 1],
                                                 ALU.mult, ALU.add).then_inc(added[q], 1)

                    staggered(dve, [(mask, 3), (make_v, 3), (new_max, 5), (add, 6)], kept.clear)

                @block.tensor
                def _(pe):
                    def turn_v(turn, q):
                        pe.wait_ge(spread_made[q], turn + 1)
                        if q >= 2:
                            pe.wait_ge(logit_made[q - 2], turn + 1)
                        elif not isinstance(turn, int) or turn:
                            pe.wait_ge(logit_made[q - 2 + RING], turn)
                        for u in range(GROUP):
                            last = nc.tensor.transpose(ps_v[:, q % 2, u * P:(u + 1) * P], spread_e[:, q, u, :], ident[:, :])
                        last.then_inc(v_turned[q], 1)

                    def turn_prob(turn, q):
                        pe.wait_ge(prob_made[q], turn + 1)
                        if q >= 2:
                            pe.wait_ge(probT_made[q - 2], turn + 2)
                        else:
                            pe.wait_ge(probT_made[q - 2 + RING], turn + 1)
                        for u in range(GROUP):
                            last = nc.tensor.transpose(ps_p[:, q % 2, u * P:(u + 1) * P], prob[:, q % 2, u, :], ident[:, :])
                        last.then_inc(prob_turned[q], 1)

                    def sum_up(turn, q):
                        if q >= RING // 2:
                            pe.wait_ge(added[q - RING // 2], turn + (turn0 + 2))
                        else:
                            pe.wait_ge(added[q + RING // 2], turn + (turn0 + 1))
                        pe.wait_ge(probT_made[q], turn + 2)
                        for u in range(GROUP):
                            last = nc.tensor.matmul(ps_o[:, q % (RING // 2), 0:DENOM + 1], probT[:, q % 2, u * P:(u + 1) * P],
                                                    gathered[:, q, u, 0:DENOM + 1], start=(u == 0), stop=(u == GROUP - 1))
                        last.then_inc(summed[q], 1)

                    staggered(pe, [(turn_v, 4), (turn_prob, 5), (sum_up, 5)])

        with ExitStack() as five:
            h = sb("h2", [P, 2, D], scope=five)
            stats = sb("stats2", [P, 6], scope=five)
            moments = sb("moments2", [P, 2, 2], scope=five)
            eps = sb("eps2", [P, 1], scope=five)
            spread = sb("spread2", [P, 2], scope=five)
            inv = sb("inv2", [P, NT], scope=five)
            vlast = sem("vlast")
            std_made = sem("std2_made")
            normed = sem("normed")
            out_stored = sem("out_stored")
            block = five.enter_context(nc.Block())

            @block.sync
            def _(sp):
                with sp.Fori(0, NT) as t:
                    sp.wait_ge(normed, t * 2 + 2)
                    sp.dma_start(out[bass.ds(t * P, P), :], acc_f[:, bass.ds(t * ROW, D)]).then_inc(out_stored, 16)
                sp.wait_ge(out_stored, NT * 16)

            @block.scalar
            def _(act):
                def make_std(t, pair, buf):
                    act.wait_ge(vlast, t * 3 + 6)
                    act.activation(spread[:, buf:buf + 1], moments[:, buf, 1:2], ACT.Sqrt, bias=eps[:, 0:1]).then_inc(std_made, 1)

                in_pairs(act, [(make_std, 0)])

            @block.vector
            def _(dve):
                dve.memset(eps[:, :], EPS).then_inc(vlast, 1)
                dve.tensor_scalar(inv[:, :], rows_b[:, :, DENOM], 1e-30, None, ALU.max).then_inc(vlast, 1)
                dve.wait_ge(vlast, 2)
                dve.reciprocal(inv[:, :], inv[:, :]).then_inc(vlast, 1)

                def add_up(t, pair, buf):
                    if not isinstance(t, int) or t >= 2:
                        dve.wait_ge(normed, t * 2 - 2)
                    rises, at = in_register(dve, t * 3 + 3), in_register(dve, t * ROW)
                    dve.wait_ge(vlast, rises)
                    dve.scalar_tensor_tensor(h[:, buf, :], acc_b[:, bass.ds(at, D)], inv[:, bass.ds(t, 1)],
                                             acc_f[:, bass.ds(at, D)], ALU.mult, ALU.add).then_inc(vlast, 1)
                    dve.wait_ge(vlast, rises + 1)
                    dve.bn_stats(stats[:, :], h[:, buf, :]).then_inc(vlast, 1)
                    dve.wait_ge(vlast, rises + 2)
                    dve.nop(nofuse=True)
                    dve.bn_aggr(moments[:, buf, :], stats[:, :]).then_inc(vlast, 1)

                def norm(t, pair, buf):
                    dve.wait_ge(std_made, t + 1)
                    dve.reciprocal(spread[:, buf:buf + 1], spread[:, buf:buf + 1]).then_inc(normed, 1)
                    dve.wait_ge(normed, t * 2 + 1)
                    dve.tensor_scalar(acc_f[:, bass.ds(t * ROW, D)], h[:, buf, :], moments[:, buf, 0:1], spread[:, buf:buf + 1],
                                      ALU.subtract, ALU.mult).then_inc(normed, 1)

                in_pairs(dve, [(add_up, 0), (norm, 1)])


_INS = ["x_pad", "xT_pad", "src", "dst", "edge_attr_64", "edge_type_16", "L0_gnn_Wf", "L0_gnn_Wb",
        "L0_gnn_loop_weight", "L0_gnn_forward_bias", "L0_gnn_backward_bias", "L0_gnn_self_bias",
        "L1_gnn_W", "L1_gnn_WT", "L1_gnn_A"]


def kernel(**inputs):
    import numpy as _np
    import concourse.bacc as _bacc
    from concourse import mybir as _mybir
    from concourse.bass_utils import run_bass_kernel_spmd as _run

    n, d = inputs["x"].shape
    n_pad = -(-n // 128) * 128
    x_pad = _np.zeros((n_pad, d), _np.float32)
    x_pad[:n] = inputs["x"]
    laid = dict(inputs)
    laid["x_pad"] = x_pad
    laid["xT_pad"] = x_pad.T
    laid["L1_gnn_WT"] = _np.asarray(inputs["L1_gnn_W"]).T

    nc = _bacc.Bacc("TRN2", target_bir_lowering=False, num_devices=1)
    arrays, args = {}, []
    for name in _INS:
        a = _np.ascontiguousarray(laid[name])
        arrays[f"in_{name}_dram"] = a
        args.append(nc.dram_tensor(f"in_{name}_dram", a.shape, _mybir.dt.from_np(a.dtype), kind="ExternalInput").ap())
    out = nc.dram_tensor("out_0_dram", (n_pad, d), _mybir.dt.float32, kind="ExternalOutput").ap()
    gnn(nc, *args, out)
    r = _run(nc, [arrays], core_ids=[0])
    return r.results[0]["out_0_dram"][:n]
```
